# Optimizing a Trainium2 kernel written in Bass

```python
import numpy as np
import jax
import jax.numpy as jnp

def _softmax(x, axis=-1):
    return jax.nn.softmax(x, axis=axis)

def _gelu(x):
    return jax.nn.gelu(x, approximate=True)

def _silu(x):
    return jax.nn.silu(x)

def _sigmoid(x):
    return jax.nn.sigmoid(x)

def _layernorm(x, axis=-1, eps=1e-05):
    m = jnp.mean(x, axis=axis, keepdims=True)
    v = jnp.var(x, axis=axis, keepdims=True)
    return (x - m) / jnp.sqrt(v + eps)

def _scatter_add(tgt, idx, src, axis=0):
    return tgt.at[idx].add(src)

def _segment_sum(src, seg, n):
    return jax.ops.segment_sum(src, seg, n)
kernel_name = 'mk_lm_tower_d4_tok_ids256_r4_b9722d'

def setup_inputs(seed: int=0):
    np.random.seed(seed)
    _w = jnp.asarray

    def _rec_inputs():
        import jax
        import jax.numpy as jnp
        _rk = jax.random.key(seed)
        x = jax.random.randint(jax.random.fold_in(_rk, 1), (4, 512), 0, 100, jnp.int32)
        mask_BSS_b0_1 = jnp.logical_not(jnp.ones((4, 512, 512), dtype=bool))
        fside_BSS_rel_dist = jax.random.uniform(jax.random.fold_in(_rk, 22), (4, 512, 512), jnp.float32, 0.0, 1)
        return (x, mask_BSS_b0_1, fside_BSS_rel_dist)
    x, mask_BSS_b0_1, fside_BSS_rel_dist = _rec_inputs()

    def _L0_tok_setup():
        import jax, jax.numpy as jnp
        import numpy as np
        NUM_ATOMS = 100
        DIM = 64
        LN_EPS = 1e-05
        key = jax.random.key(seed)
        ks = jax.random.split(key, 10)
        b, n, d = (4, 512, DIM)
        atom_ids = jax.random.randint(ks[0], (b, n), 0, NUM_ATOMS)
        adj_mat = jax.random.randint(ks[1], (b, n, n), 0, 2).astype(bool)
        rel_dist = jax.random.uniform(ks[2], (b, n, n), dtype=jnp.float32)
        s = 1.0 / np.sqrt(d)
        params = {'atom_embed': jax.random.normal(ks[3], (NUM_ATOMS, d), jnp.float32), 'neighbor_embed': jax.random.normal(ks[4], (NUM_ATOMS, d), jnp.float32), 'w_rd': jax.random.normal(ks[5], (d,), jnp.float32), 'w1': jax.random.normal(ks[6], (2 * d, d), jnp.float32) * s, 'b1': jnp.zeros((d,), jnp.float32), 'gamma': jnp.ones((d,), jnp.float32), 'beta': jnp.zeros((d,), jnp.float32), 'w2': jax.random.normal(ks[7], (d, d), jnp.float32) * s, 'b2': jnp.zeros((d,), jnp.float32)}
        return {'atom_ids': atom_ids, 'adj_mat': adj_mat, 'rel_dist': rel_dist, **params}
    _L0_tok_all = _L0_tok_setup()
    _L0_tok_in = {k: v for k, v in _L0_tok_all.items() if k in ('atom_embed', 'neighbor_embed', 'w_rd', 'w1', 'b1', 'gamma', 'beta', 'w2', 'b2')}
    del _L0_tok_all

    def _L0_attn_setup():
        import jax, jax.numpy as jnp
        import numpy as np
        EPS = 1e-09

        def _glorot(key, shape):
            fan_in, fan_out = (shape[-2], shape[-1])
            std = (2.0 / (fan_in + fan_out)) ** 0.5
            return jax.random.normal(key, shape, dtype=jnp.float32) * std

        def _reference_tuple_inner(x, Wks, Wqs, Wvs, Wo):
            keys = jnp.einsum('bsd,hdk->hbsk', x, Wks)
            queries = jnp.einsum('bsd,hdk->hbsk', x, Wqs)
            values = jnp.einsum('bsd,hde->hbse', x, Wvs)
            keys = jax.nn.elu(keys) + 1.0
            queries = jax.nn.elu(queries) + 1.0
            att = jnp.einsum('hbsk,hbtk->hbst', queries, keys)
            S = att.shape[-1]
            causal = jnp.tril(jnp.ones((S, S), dtype=att.dtype))
            att = att * causal
            att = att / (jnp.sum(att, axis=-1, keepdims=True) + EPS)
            kv = jnp.einsum('hbsk,hbsd->hbsdk', keys, values)
            kv_cum = jnp.cumsum(kv, axis=2)
            numerator = jnp.einsum('hbsdk,hbsk->hbsd', kv_cum, queries)
            denominator = jnp.einsum('hbsk,hbsk->hbs', jnp.cumsum(keys, axis=2), queries)
            node = numerator / (denominator[..., None] + EPS)
            out = jnp.einsum('hbsd,hde->bse', node, Wo)
            return (out, att)
        key = jax.random.key(seed)
        kx, k1, k2, k3, k4 = jax.random.split(key, 5)
        B, S, D = (2, 256, 64)
        H, K = (8, 32)
        return {'x': jax.random.normal(kx, (B, S, D), dtype=jnp.float32), 'Wks': _glorot(k1, (H, D, K)), 'Wqs': _glorot(k2, (H, D, K)), 'Wvs': _glorot(k3, (H, D, D)), 'Wo': _glorot(k4, (H, D, D))}
    _L0_attn_all = _L0_attn_setup()
    _L0_attn_in = {k: v for k, v in _L0_attn_all.items() if k in ('Wks', 'Wqs', 'Wvs', 'Wo')}
    del _L0_attn_all

    def _L0_ffn_setup():
        import jax, jax.numpy as jnp
        import numpy as np
        B, S, H, F, E, K = (8, 1024, 64, 128, 16, 2)
        EPS = 1e-05
        key = jax.random.key(seed)
        ks = jax.random.split(key, 9)
        sc = 0.02
        return {'x': jax.random.normal(ks[0], (B, S, H), dtype=jnp.float32), 'gate_w': jax.random.normal(ks[1], (H, E), dtype=jnp.float32) * sc, 'gate_b': jnp.zeros((E,), dtype=jnp.float32), 'w1': jax.random.normal(ks[2], (E, H, F), dtype=jnp.float32) * sc, 'b1': jnp.zeros((E, F), dtype=jnp.float32), 'w2': jax.random.normal(ks[3], (E, F, H), dtype=jnp.float32) * sc, 'b2': jnp.zeros((E, H), dtype=jnp.float32), 'gamma': jnp.ones((H,), dtype=jnp.float32), 'beta': jnp.zeros((H,), dtype=jnp.float32)}
    _L0_ffn_all = _L0_ffn_setup()
    _L0_ffn_in = {k: v for k, v in _L0_ffn_all.items() if k in ('gate_w', 'gate_b', 'w1', 'b1', 'w2', 'b2', 'gamma', 'beta')}
    del _L0_ffn_all

    def _L1_attn_setup():
        import jax, jax.numpy as jnp
        import numpy as np
        B, N, D = (8, 512, 64)
        key = jax.random.key(seed)
        k1, k2, k3, k4 = jax.random.split(key, 4)
        s = D ** (-0.5)
        return {'x': jax.random.normal(k1, (B, N, D), dtype=jnp.float32), 'Wq': jax.random.normal(k2, (D, D), dtype=jnp.float32) * s, 'Wk': jax.random.normal(k3, (D, D), dtype=jnp.float32) * s, 'Wv': jax.random.normal(k4, (D, D), dtype=jnp.float32) * s}
    _L1_attn_all = _L1_attn_setup()
    _L1_attn_in = {k: v for k, v in _L1_attn_all.items() if k in ('Wq', 'Wk', 'Wv')}
    del _L1_attn_all

    def _L1_ffn_setup():
        import jax, jax.numpy as jnp
        import numpy as np
        B, N, D = (16, 1024, 64)
        NUM_EXPERTS, TOP_K, HEADS = (4, 2, 4)
        N_EDGES = 262144
        LN_EPS = 1e-05

        def _layernorm(x, g, b):
            mu = x.mean(-1, keepdims=True)
            var = ((x - mu) ** 2).mean(-1, keepdims=True)
            return (x - mu) * jax.lax.rsqrt(var + LN_EPS) * g + b

        def _forward(x, edge_index, W_gat, att_src, att_dst, b_gat, ln_gamma, ln_beta, W1, b1, W2, b2):
            Bc, Nc, Dc = x.shape
            M = Bc * Nc
            x_flat = x.reshape(M, Dc)
            h = (x_flat @ W_gat).reshape(M, HEADS, NUM_EXPERTS)
            loops = jnp.arange(M, dtype=edge_index.dtype)
            src = jnp.concatenate([edge_index[0], loops])
            dst = jnp.concatenate([edge_index[1], loops])
            a_src = (h * att_src).sum(-1)
            a_dst = (h * att_dst).sum(-1)
            e = jax.nn.leaky_relu(a_src[src] + a_dst[dst], negative_slope=0.2)
            e_max = jax.ops.segment_max(e, dst, num_segments=M)
            ee = jnp.exp(e - e_max[dst])
            denom = jax.ops.segment_sum(ee, dst, num_segments=M)
            alpha = ee / (denom[dst] + 1e-16)
            msg = h[src] * alpha[:, :, None]
            agg = jax.ops.segment_sum(msg, dst, num_segments=M).reshape(M, HEADS * NUM_EXPERTS) + b_gat
            scores = _layernorm(agg, ln_gamma, ln_beta).reshape(M, HEADS, NUM_EXPERTS).mean(1)
            scores = scores.reshape(Bc, Nc, NUM_EXPERTS)
            topk_s, topk_i = jax.lax.top_k(scores, TOP_K)
            w = jax.nn.softmax(topk_s, axis=-1)
            out = jnp.zeros_like(x)
            for ei in range(NUM_EXPERTS):
                g = jnp.where(topk_i == ei, w, 0.0).sum(-1)
                hh = jax.nn.gelu(x @ W1[ei] + b1[ei], approximate=False)
                out = out + g[..., None] * (hh @ W2[ei] + b2[ei])
            return out
        key = jax.random.key(seed)
        ks = jax.random.split(key, 8)
        s = 0.05
        return {'x': jax.random.normal(ks[0], (B, N, D), jnp.float32), 'W_gat': jax.random.normal(ks[1], (D, HEADS * NUM_EXPERTS), jnp.float32) * s, 'att_src': jax.random.normal(ks[2], (HEADS, NUM_EXPERTS), jnp.float32) * s, 'att_dst': jax.random.normal(ks[3], (HEADS, NUM_EXPERTS), jnp.float32) * s, 'b_gat': jnp.zeros((HEADS * NUM_EXPERTS,), jnp.float32), 'ln_gamma': jnp.ones((HEADS * NUM_EXPERTS,), jnp.float32), 'ln_beta': jnp.zeros((HEADS * NUM_EXPERTS,), jnp.float32), 'W1': jax.random.normal(ks[4], (NUM_EXPERTS, D, 2 * D), jnp.float32) * s, 'b1': jnp.zeros((NUM_EXPERTS, 2 * D), jnp.float32), 'W2': jax.random.normal(ks[5], (NUM_EXPERTS, 2 * D, D), jnp.float32) * s, 'b2': jnp.zeros((NUM_EXPERTS, D), jnp.float32), 'edge_index': jax.random.randint(ks[6], (2, N_EDGES), 0, B * N, jnp.int32)}
    _L1_ffn_all = _L1_ffn_setup()
    _L1_ffn_in = {k: v for k, v in _L1_ffn_all.items() if k in ('W_gat', 'att_src', 'att_dst', 'b_gat', 'ln_gamma', 'ln_beta', 'W1', 'b1', 'W2', 'b2', 'edge_index')}
    del _L1_ffn_all

    def _L2_attn_setup():
        import jax, jax.numpy as jnp
        import numpy as np
        MIDC = 64
        HEADS = 16
        HEADC = MIDC // HEADS
        EPS = 1e-05

        def _layernorm(x, w, b):
            mean = jnp.mean(x, axis=-1, keepdims=True)
            std = jnp.std(x, axis=-1, keepdims=True, ddof=1)
            return w * (x - mean) / (std + EPS) + b
        key = jax.random.key(seed)
        ks = jax.random.split(key, 3)
        B, HW = (8, 4096)
        x = jax.random.normal(ks[0], (B, HW, MIDC), dtype=jnp.float32)
        W_qkv = jax.random.normal(ks[1], (3 * MIDC, MIDC), dtype=jnp.float32) * 0.02
        b_qkv = jnp.zeros((3 * MIDC,), dtype=jnp.float32)
        kln_w = jnp.ones((HEADS, 1, HEADC), dtype=jnp.float32)
        kln_b = jnp.zeros((HEADS, 1, HEADC), dtype=jnp.float32)
        vln_w = jnp.ones((HEADS, 1, HEADC), dtype=jnp.float32)
        vln_b = jnp.zeros((HEADS, 1, HEADC), dtype=jnp.float32)
        W_proj = jax.random.normal(ks[2], (MIDC, MIDC), dtype=jnp.float32) * 0.02
        b_proj = jnp.zeros((MIDC,), dtype=jnp.float32)
        return {'x': x, 'W_qkv': W_qkv, 'b_qkv': b_qkv, 'kln_w': kln_w, 'kln_b': kln_b, 'vln_w': vln_w, 'vln_b': vln_b, 'W_proj': W_proj, 'b_proj': b_proj}
    _L2_attn_all = _L2_attn_setup()
    _L2_attn_in = {k: v for k, v in _L2_attn_all.items() if k in ('W_qkv', 'b_qkv', 'kln_w', 'kln_b', 'vln_w', 'vln_b', 'W_proj', 'b_proj')}
    del _L2_attn_all

    def _L2_ffn_setup():
        import jax, jax.numpy as jnp
        import numpy as np
        NUM_EXPERTS = 8
        TOP_K = 2
        B, S, D = (8, 2048, 64)

        def _moe(tokens, router_w, w1, b1, w2, b2):
            N = tokens.shape[0]
            E = router_w.shape[0]
            logits = tokens.astype(jnp.float32) @ router_w.astype(jnp.float32).T
            probs = jax.nn.softmax(logits, axis=-1)
            rw, re = jax.lax.top_k(probs, TOP_K)
            if TOP_K > 1:
                rw = rw / jnp.maximum(rw.sum(-1, keepdims=True), 1e-12)
            rw = rw.astype(tokens.dtype)
            combine = jnp.zeros((N, E), tokens.dtype).at[jnp.arange(N)[:, None], re].set(rw)
            out = tokens
            for e in range(E):
                h = jax.nn.gelu(tokens @ w1[e] + b1[e], approximate=False)
                y = h @ w2[e] + b2[e]
                out = out + combine[:, e:e + 1] * y
            return out
        key = jax.random.key(seed)
        ks = jax.random.split(key, 4)
        scale = 1.0 / np.sqrt(D).astype(np.float32)
        return {'input_embeddings': jax.random.normal(ks[0], (B, S, D), jnp.float32), 'router_w': jax.random.normal(ks[1], (NUM_EXPERTS, D), jnp.float32) * scale, 'w1': jax.random.normal(ks[2], (NUM_EXPERTS, D, D), jnp.float32) * scale, 'b1': jnp.zeros((NUM_EXPERTS, D), jnp.float32), 'w2': jax.random.normal(ks[3], (NUM_EXPERTS, D, D), jnp.float32) * scale, 'b2': jnp.zeros((NUM_EXPERTS, D), jnp.float32)}
    _L2_ffn_all = _L2_ffn_setup()
    _L2_ffn_in = {k: v for k, v in _L2_ffn_all.items() if k in ('router_w', 'w1', 'b1', 'w2', 'b2')}
    del _L2_ffn_all

    def _L3_attn_setup():
        import jax, jax.numpy as jnp
        import numpy as np
        from math import sqrt
        DIM = 64
        key = jax.random.key(seed)
        k1, k2, k3, k4 = jax.random.split(key, 4)
        B, T, D, H, R = (2, 1024, DIM, 8, 32)

        def xavier(k, shape, fan_in, fan_out):
            a = sqrt(6.0 / (fan_in + fan_out))
            return jax.random.uniform(k, shape, jnp.float32, -a, a)
        x = jax.random.normal(k1, (B, T, D), jnp.float32)
        Q = xavier(k2, (H, R, D), D, R)
        K = xavier(k3, (H, R, D), D, R)
        VO = xavier(k4, (H, D, D), D, D)
        return {'x': x, 'Q': Q, 'K': K, 'VO': VO}
    _L3_attn_all = _L3_attn_setup()
    _L3_attn_in = {k: v for k, v in _L3_attn_all.items() if k in ('Q', 'K', 'VO')}
    del _L3_attn_all

    def _L3_ffn_setup():
        import jax, jax.numpy as jnp
        import numpy as np
        B, T, C = (64, 96, 64)
        NH, NKV = (4, 2)
        HD = C // NH
        NREP = NH // NKV
        NE, TOPK = (8, 2)
        HID = int(8 / 3 * C)
        EPS_RMS = 1e-06

        def _rope_tables(t_len):
            inv_freq = 1.0 / 10000.0 ** (np.arange(0, HD, 2, dtype=np.float32) / HD)
            t = np.arange(t_len, dtype=np.float32)
            freqs = np.outer(t, inv_freq)
            emb = np.concatenate([freqs, freqs], axis=-1)
            return (jnp.asarray(np.cos(emb)), jnp.asarray(np.sin(emb)))

        def _rotate_half(x):
            h = x.shape[-1] // 2
            return jnp.concatenate([-x[..., h:], x[..., :h]], axis=-1)

        def _rmsnorm(v, w):
            return v * jax.lax.rsqrt(jnp.mean(v * v, axis=-1, keepdims=True) + EPS_RMS) * w
        key = jax.random.key(seed)
        ks = jax.random.split(key, 10)
        s = lambda k, shape: jax.random.normal(k, shape, jnp.float32) * 0.02
        return {'x': jax.random.normal(ks[0], (B, T, C), jnp.float32), 'ln1_w': jnp.ones((C,), jnp.float32), 'ln2_w': jnp.ones((C,), jnp.float32), 'wq': s(ks[1], (NH * HD, C)), 'wk': s(ks[2], (NKV * HD, C)), 'wv': s(ks[3], (NKV * HD, C)), 'wo': s(ks[4], (C, C)), 'router_w': s(ks[5], (NE, C)), 'w1': s(ks[6], (NE, HID, C)), 'w2': s(ks[7], (NE, C, HID)), 'w3': s(ks[8], (NE, HID, C))}
    _L3_ffn_all = _L3_ffn_setup()
    _L3_ffn_in = {k: v for k, v in _L3_ffn_all.items() if k in ('ln1_w', 'ln2_w', 'wq', 'wk', 'wv', 'wo', 'router_w', 'w1', 'w2', 'w3')}
    del _L3_ffn_all
    return {'x': x, 'mask_BSS_b0_1': mask_BSS_b0_1, 'fside_BSS_rel_dist': fside_BSS_rel_dist, 'L0_tok_atom_embed': _L0_tok_in['atom_embed'], 'L0_tok_neighbor_embed': _L0_tok_in['neighbor_embed'], 'L0_tok_w_rd': _L0_tok_in['w_rd'], 'L0_tok_w1': _L0_tok_in['w1'], 'L0_tok_b1': _L0_tok_in['b1'], 'L0_tok_gamma': _L0_tok_in['gamma'], 'L0_tok_beta': _L0_tok_in['beta'], 'L0_tok_w2': _L0_tok_in['w2'], 'L0_tok_b2': _L0_tok_in['b2'], 'L0_attn_Wks': _L0_attn_in['Wks'], 'L0_attn_Wqs': _L0_attn_in['Wqs'], 'L0_attn_Wvs': _L0_attn_in['Wvs'], 'L0_attn_Wo': _L0_attn_in['Wo'], 'L0_ffn_gate_w': _L0_ffn_in['gate_w'], 'L0_ffn_gate_b': _L0_ffn_in['gate_b'], 'L0_ffn_w1': _L0_ffn_in['w1'], 'L0_ffn_b1': _L0_ffn_in['b1'], 'L0_ffn_w2': _L0_ffn_in['w2'], 'L0_ffn_b2': _L0_ffn_in['b2'], 'L0_ffn_gamma': _L0_ffn_in['gamma'], 'L0_ffn_beta': _L0_ffn_in['beta'], 'L1_attn_Wq': _L1_attn_in['Wq'], 'L1_attn_Wk': _L1_attn_in['Wk'], 'L1_attn_Wv': _L1_attn_in['Wv'], 'L1_ffn_W_gat': _L1_ffn_in['W_gat'], 'L1_ffn_att_src': _L1_ffn_in['att_src'], 'L1_ffn_att_dst': _L1_ffn_in['att_dst'], 'L1_ffn_b_gat': _L1_ffn_in['b_gat'], 'L1_ffn_ln_gamma': _L1_ffn_in['ln_gamma'], 'L1_ffn_ln_beta': _L1_ffn_in['ln_beta'], 'L1_ffn_W1': _L1_ffn_in['W1'], 'L1_ffn_b1': _L1_ffn_in['b1'], 'L1_ffn_W2': _L1_ffn_in['W2'], 'L1_ffn_b2': _L1_ffn_in['b2'], 'L1_ffn_edge_index': _L1_ffn_in['edge_index'], 'L2_attn_W_qkv': _L2_attn_in['W_qkv'], 'L2_attn_b_qkv': _L2_attn_in['b_qkv'], 'L2_attn_kln_w': _L2_attn_in['kln_w'], 'L2_attn_kln_b': _L2_attn_in['kln_b'], 'L2_attn_vln_w': _L2_attn_in['vln_w'], 'L2_attn_vln_b': _L2_attn_in['vln_b'], 'L2_attn_W_proj': _L2_attn_in['W_proj'], 'L2_attn_b_proj': _L2_attn_in['b_proj'], 'L2_ffn_router_w': _L2_ffn_in['router_w'], 'L2_ffn_w1': _L2_ffn_in['w1'], 'L2_ffn_b1': _L2_ffn_in['b1'], 'L2_ffn_w2': _L2_ffn_in['w2'], 'L2_ffn_b2': _L2_ffn_in['b2'], 'L3_attn_Q': _L3_attn_in['Q'], 'L3_attn_K': _L3_attn_in['K'], 'L3_attn_VO': _L3_attn_in['VO'], 'L3_ffn_ln1_w': _L3_ffn_in['ln1_w'], 'L3_ffn_ln2_w': _L3_ffn_in['ln2_w'], 'L3_ffn_wq': _L3_ffn_in['wq'], 'L3_ffn_wk': _L3_ffn_in['wk'], 'L3_ffn_wv': _L3_ffn_in['wv'], 'L3_ffn_wo': _L3_ffn_in['wo'], 'L3_ffn_router_w': _L3_ffn_in['router_w'], 'L3_ffn_w1': _L3_ffn_in['w1'], 'L3_ffn_w2': _L3_ffn_in['w2'], 'L3_ffn_w3': _L3_ffn_in['w3']}

def reference(x, mask_BSS_b0_1, fside_BSS_rel_dist, L0_tok_atom_embed, L0_tok_neighbor_embed, L0_tok_w_rd, L0_tok_w1, L0_tok_b1, L0_tok_gamma, L0_tok_beta, L0_tok_w2, L0_tok_b2, L0_attn_Wks, L0_attn_Wqs, L0_attn_Wvs, L0_attn_Wo, L0_ffn_gate_w, L0_ffn_gate_b, L0_ffn_w1, L0_ffn_b1, L0_ffn_w2, L0_ffn_b2, L0_ffn_gamma, L0_ffn_beta, L1_attn_Wq, L1_attn_Wk, L1_attn_Wv, L1_ffn_W_gat, L1_ffn_att_src, L1_ffn_att_dst, L1_ffn_b_gat, L1_ffn_ln_gamma, L1_ffn_ln_beta, L1_ffn_W1, L1_ffn_b1, L1_ffn_W2, L1_ffn_b2, L1_ffn_edge_index, L2_attn_W_qkv, L2_attn_b_qkv, L2_attn_kln_w, L2_attn_kln_b, L2_attn_vln_w, L2_attn_vln_b, L2_attn_W_proj, L2_attn_b_proj, L2_ffn_router_w, L2_ffn_w1, L2_ffn_b1, L2_ffn_w2, L2_ffn_b2, L3_attn_Q, L3_attn_K, L3_attn_VO, L3_ffn_ln1_w, L3_ffn_ln2_w, L3_ffn_wq, L3_ffn_wk, L3_ffn_wv, L3_ffn_wo, L3_ffn_router_w, L3_ffn_w1, L3_ffn_w2, L3_ffn_w3):
    import jax
    import jax.numpy as jnp

    def _L0_tok_ref(atom_ids, adj_mat, rel_dist, atom_embed, neighbor_embed, w_rd, w1, b1, gamma, beta, w2, b2):
        import jax, jax.numpy as jnp
        import numpy as np
        NUM_ATOMS = 100
        DIM = 64
        LN_EPS = 1e-05
        n = atom_ids.shape[-1]
        eye = jnp.eye(n, dtype=bool)
        mask = adj_mat & ~eye
        embeds = atom_embed[atom_ids]
        nbr_embeds = neighbor_embed[atom_ids]
        weighted = jnp.where(mask, rel_dist, jnp.zeros((), rel_dist.dtype))
        neighbor_feats = jnp.einsum('bij,bjd->bid', weighted, nbr_embeds) * w_rd
        x = jnp.concatenate([embeds, neighbor_feats], axis=-1)
        h = x @ w1 + b1
        mu = jnp.mean(h, axis=-1, keepdims=True)
        var = jnp.mean(jnp.square(h - mu), axis=-1, keepdims=True)
        h = (h - mu) * jax.lax.rsqrt(var + LN_EPS) * gamma + beta
        h = jax.nn.silu(h)
        return h @ w2 + b2

    def _L0_attn_ref(x, Wks, Wqs, Wvs, Wo):
        import jax, jax.numpy as jnp
        import numpy as np
        EPS = 1e-09

        def _glorot(key, shape):
            fan_in, fan_out = (shape[-2], shape[-1])
            std = (2.0 / (fan_in + fan_out)) ** 0.5
            return jax.random.normal(key, shape, dtype=jnp.float32) * std

        def _reference_tuple_inner(x, Wks, Wqs, Wvs, Wo):
            keys = jnp.einsum('bsd,hdk->hbsk', x, Wks)
            queries = jnp.einsum('bsd,hdk->hbsk', x, Wqs)
            values = jnp.einsum('bsd,hde->hbse', x, Wvs)
            keys = jax.nn.elu(keys) + 1.0
            queries = jax.nn.elu(queries) + 1.0
            att = jnp.einsum('hbsk,hbtk->hbst', queries, keys)
            S = att.shape[-1]
            causal = jnp.tril(jnp.ones((S, S), dtype=att.dtype))
            att = att * causal
            att = att / (jnp.sum(att, axis=-1, keepdims=True) + EPS)
            kv = jnp.einsum('hbsk,hbsd->hbsdk', keys, values)
            kv_cum = jnp.cumsum(kv, axis=2)
            numerator = jnp.einsum('hbsdk,hbsk->hbsd', kv_cum, queries)
            denominator = jnp.einsum('hbsk,hbsk->hbs', jnp.cumsum(keys, axis=2), queries)
            node = numerator / (denominator[..., None] + EPS)
            out = jnp.einsum('hbsd,hde->bse', node, Wo)
            return (out, att)
        return _reference_tuple_inner(x, Wks, Wqs, Wvs, Wo)[0]

    def _L0_ffn_ref(x, gate_w, gate_b, w1, b1, w2, b2, gamma, beta):
        import jax, jax.numpy as jnp
        import numpy as np
        B, S, H, F, E, K = (8, 1024, 64, 128, 16, 2)
        EPS = 1e-05
        gate_logits = x @ gate_w + gate_b
        topk_vals, topk_idx = jax.lax.top_k(gate_logits, K)
        topk_w = jax.nn.softmax(topk_vals, axis=-1)
        h = jax.nn.relu(jnp.einsum('bsh,ehf->bsef', x, w1) + b1)
        expert_out = jnp.einsum('bsef,efh->bseh', h, w2) + b2
        sel = jnp.take_along_axis(expert_out, topk_idx[:, :, :, None], axis=2)
        moe = jnp.sum(topk_w[..., None] * sel, axis=2)
        y = x + moe
        mu = jnp.mean(y, axis=-1, keepdims=True)
        var = jnp.var(y, axis=-1, keepdims=True)
        return (y - mu) / jnp.sqrt(var + EPS) * gamma + beta

    def _L1_attn_ref(x, Wq, Wk, Wv):
        import jax, jax.numpy as jnp
        import numpy as np
        B, N, D = (8, 512, 64)
        q = jnp.einsum('bnd,ed->bne', x, Wq)
        k = jnp.einsum('bnd,ed->bne', x, Wk)
        v = jnp.einsum('bnd,ed->bne', x, Wv)
        energy = jnp.einsum('bqd,bkd->bqk', q, k)
        scaling = jnp.asarray(x.shape[-1] ** (-0.5), x.dtype)
        att = jax.nn.softmax(energy, axis=-1) * scaling
        out = jnp.einsum('bqk,bkv->bqv', att, v)
        return out

    def _L1_ffn_ref(x, W_gat, att_src, att_dst, b_gat, ln_gamma, ln_beta, W1, b1, W2, b2, edge_index):
        import jax, jax.numpy as jnp
        import numpy as np
        B, N, D = (16, 1024, 64)
        NUM_EXPERTS, TOP_K, HEADS = (4, 2, 4)
        N_EDGES = 262144
        LN_EPS = 1e-05

        def _layernorm(x, g, b):
            mu = x.mean(-1, keepdims=True)
            var = ((x - mu) ** 2).mean(-1, keepdims=True)
            return (x - mu) * jax.lax.rsqrt(var + LN_EPS) * g + b

        def _forward(x, edge_index, W_gat, att_src, att_dst, b_gat, ln_gamma, ln_beta, W1, b1, W2, b2):
            Bc, Nc, Dc = x.shape
            M = Bc * Nc
            x_flat = x.reshape(M, Dc)
            h = (x_flat @ W_gat).reshape(M, HEADS, NUM_EXPERTS)
            loops = jnp.arange(M, dtype=edge_index.dtype)
            src = jnp.concatenate([edge_index[0], loops])
            dst = jnp.concatenate([edge_index[1], loops])
            a_src = (h * att_src).sum(-1)
            a_dst = (h * att_dst).sum(-1)
            e = jax.nn.leaky_relu(a_src[src] + a_dst[dst], negative_slope=0.2)
            e_max = jax.ops.segment_max(e, dst, num_segments=M)
            ee = jnp.exp(e - e_max[dst])
            denom = jax.ops.segment_sum(ee, dst, num_segments=M)
            alpha = ee / (denom[dst] + 1e-16)
            msg = h[src] * alpha[:, :, None]
            agg = jax.ops.segment_sum(msg, dst, num_segments=M).reshape(M, HEADS * NUM_EXPERTS) + b_gat
            scores = _layernorm(agg, ln_gamma, ln_beta).reshape(M, HEADS, NUM_EXPERTS).mean(1)
            scores = scores.reshape(Bc, Nc, NUM_EXPERTS)
            topk_s, topk_i = jax.lax.top_k(scores, TOP_K)
            w = jax.nn.softmax(topk_s, axis=-1)
            out = jnp.zeros_like(x)
            for ei in range(NUM_EXPERTS):
                g = jnp.where(topk_i == ei, w, 0.0).sum(-1)
                hh = jax.nn.gelu(x @ W1[ei] + b1[ei], approximate=False)
                out = out + g[..., None] * (hh @ W2[ei] + b2[ei])
            return out
        return _forward(x, edge_index, W_gat, att_src, att_dst, b_gat, ln_gamma, ln_beta, W1, b1, W2, b2)

    def _L2_attn_ref(x, W_qkv, b_qkv, kln_w, kln_b, vln_w, vln_b, W_proj, b_proj):
        import jax, jax.numpy as jnp
        import numpy as np
        MIDC = 64
        HEADS = 16
        HEADC = MIDC // HEADS
        EPS = 1e-05

        def _layernorm(x, w, b):
            mean = jnp.mean(x, axis=-1, keepdims=True)
            std = jnp.std(x, axis=-1, keepdims=True, ddof=1)
            return w * (x - mean) / (std + EPS) + b
        B, HW, C = x.shape
        bias = x
        qkv = jnp.einsum('bnc,oc->bno', x, W_qkv) + b_qkv
        qkv = qkv.reshape(B, HW, HEADS, 3 * HEADC).transpose(0, 2, 1, 3)
        q, k, v = jnp.split(qkv, 3, axis=-1)
        k = _layernorm(k, kln_w, kln_b)
        v = _layernorm(v, vln_w, vln_b)
        kv = jnp.einsum('bhnd,bhne->bhde', k, v) / HW
        out = jnp.einsum('bhnd,bhde->bhne', q, kv)
        out = out.transpose(0, 2, 1, 3).reshape(B, HW, C)
        ret = out + bias
        proj = jnp.einsum('bnc,oc->bno', ret, W_proj) + b_proj
        return jax.nn.gelu(proj, approximate=False) + bias

    def _L2_ffn_ref(input_embeddings, router_w, w1, b1, w2, b2):
        import jax, jax.numpy as jnp
        import numpy as np
        NUM_EXPERTS = 8
        TOP_K = 2
        B, S, D = (8, 2048, 64)

        def _moe(tokens, router_w, w1, b1, w2, b2):
            N = tokens.shape[0]
            E = router_w.shape[0]
            logits = tokens.astype(jnp.float32) @ router_w.astype(jnp.float32).T
            probs = jax.nn.softmax(logits, axis=-1)
            rw, re = jax.lax.top_k(probs, TOP_K)
            if TOP_K > 1:
                rw = rw / jnp.maximum(rw.sum(-1, keepdims=True), 1e-12)
            rw = rw.astype(tokens.dtype)
            combine = jnp.zeros((N, E), tokens.dtype).at[jnp.arange(N)[:, None], re].set(rw)
            out = tokens
            for e in range(E):
                h = jax.nn.gelu(tokens @ w1[e] + b1[e], approximate=False)
                y = h @ w2[e] + b2[e]
                out = out + combine[:, e:e + 1] * y
            return out
        b, s, d = input_embeddings.shape
        tokens = input_embeddings.reshape(b * s, d)
        return _moe(tokens, router_w, w1, b1, w2, b2).reshape(b, s, d)

    def _L3_attn_ref(x, Q, K, VO):
        import jax, jax.numpy as jnp
        import numpy as np
        from math import sqrt
        DIM = 64
        d = x.shape[-1]
        q = jnp.einsum('btd,hrd->bhtr', x, Q)
        k = jnp.einsum('bud,hrd->bhur', x, K)
        scores = jnp.einsum('bhtr,bhur->bhtu', q, k) / sqrt(d)
        attn = jax.nn.softmax(scores, axis=-1)
        ctx = jnp.einsum('bhtu,bud->bhtd', attn, x)
        out = jnp.einsum('bhtd,hde->bte', ctx, VO)
        return out

    def _L3_ffn_ref(x, ln1_w, ln2_w, wq, wk, wv, wo, router_w, w1, w2, w3):
        import jax, jax.numpy as jnp
        import numpy as np
        B, T, C = (64, 96, 64)
        NH, NKV = (4, 2)
        HD = C // NH
        NREP = NH // NKV
        NE, TOPK = (8, 2)
        HID = int(8 / 3 * C)
        EPS_RMS = 1e-06

        def _rope_tables(t_len):
            inv_freq = 1.0 / 10000.0 ** (np.arange(0, HD, 2, dtype=np.float32) / HD)
            t = np.arange(t_len, dtype=np.float32)
            freqs = np.outer(t, inv_freq)
            emb = np.concatenate([freqs, freqs], axis=-1)
            return (jnp.asarray(np.cos(emb)), jnp.asarray(np.sin(emb)))

        def _rotate_half(x):
            h = x.shape[-1] // 2
            return jnp.concatenate([-x[..., h:], x[..., :h]], axis=-1)

        def _rmsnorm(v, w):
            return v * jax.lax.rsqrt(jnp.mean(v * v, axis=-1, keepdims=True) + EPS_RMS) * w
        Bx, Tx, Cx = x.shape
        h = _rmsnorm(x, ln1_w)
        q = (h @ wq.T).reshape(Bx, Tx, NH, HD).transpose(0, 2, 1, 3)
        k = (h @ wk.T).reshape(Bx, Tx, NKV, HD).transpose(0, 2, 1, 3)
        v = (h @ wv.T).reshape(Bx, Tx, NKV, HD).transpose(0, 2, 1, 3)
        cos, sin = _rope_tables(Tx)
        cos, sin = (cos[None, None], sin[None, None])
        q = q * cos + _rotate_half(q) * sin
        k = k * cos + _rotate_half(k) * sin
        k = jnp.repeat(k, NREP, axis=1)
        v = jnp.repeat(v, NREP, axis=1)
        scores = jnp.einsum('bhtd,bhsd->bhts', q, k) / jnp.sqrt(jnp.float32(HD))
        causal = jnp.tril(jnp.ones((Tx, Tx), dtype=bool))
        scores = jnp.where(causal[None, None], scores, jnp.float32(-1e+30))
        att = jax.nn.softmax(scores, axis=-1)
        y = jnp.einsum('bhts,bhsd->bhtd', att, v).transpose(0, 2, 1, 3).reshape(Bx, Tx, Cx)
        x = x + y @ wo.T
        flat = _rmsnorm(x, ln2_w).reshape(-1, Cx)
        probs = jax.nn.softmax(flat @ router_w.T, axis=-1)
        tp, ti = jax.lax.top_k(probs, TOPK)
        tp = tp / (jnp.sum(tp, axis=-1, keepdims=True) + 1e-09)
        weights = jnp.sum(tp[..., None] * jax.nn.one_hot(ti, NE, dtype=flat.dtype), axis=1)
        out = jnp.zeros_like(flat)
        for e in range(NE):
            hh = jax.nn.silu(flat @ w1[e].T) * (flat @ w3[e].T)
            out = out + weights[:, e:e + 1] * (hh @ w2[e].T)
        return x + out.reshape(Bx, Tx, Cx)
    h = _L0_tok_ref(x, mask_BSS_b0_1, fside_BSS_rel_dist, L0_tok_atom_embed, L0_tok_neighbor_embed, L0_tok_w_rd, L0_tok_w1, L0_tok_b1, L0_tok_gamma, L0_tok_beta, L0_tok_w2, L0_tok_b2)
    h = h + _L0_attn_ref(_layernorm(h, axis=-1), L0_attn_Wks, L0_attn_Wqs, L0_attn_Wvs, L0_attn_Wo)
    h = h + _L0_ffn_ref(_layernorm(h, axis=-1), L0_ffn_gate_w, L0_ffn_gate_b, L0_ffn_w1, L0_ffn_b1, L0_ffn_w2, L0_ffn_b2, L0_ffn_gamma, L0_ffn_beta)
    h = h + _L1_attn_ref(_layernorm(h, axis=-1), L1_attn_Wq, L1_attn_Wk, L1_attn_Wv)
    h = h + _L1_ffn_ref(_layernorm(h, axis=-1), L1_ffn_W_gat, L1_ffn_att_src, L1_ffn_att_dst, L1_ffn_b_gat, L1_ffn_ln_gamma, L1_ffn_ln_beta, L1_ffn_W1, L1_ffn_b1, L1_ffn_W2, L1_ffn_b2, L1_ffn_edge_index)
    h = h + _L2_attn_ref(_layernorm(h, axis=-1), L2_attn_W_qkv, L2_attn_b_qkv, L2_attn_kln_w, L2_attn_kln_b, L2_attn_vln_w, L2_attn_vln_b, L2_attn_W_proj, L2_attn_b_proj)
    h = h + _L2_ffn_ref(_layernorm(h, axis=-1), L2_ffn_router_w, L2_ffn_w1, L2_ffn_b1, L2_ffn_w2, L2_ffn_b2)
    h = h + _L3_attn_ref(_layernorm(h, axis=-1), L3_attn_Q, L3_attn_K, L3_attn_VO)
    h = h + _L3_ffn_ref(_layernorm(h, axis=-1), L3_ffn_ln1_w, L3_ffn_ln2_w, L3_ffn_wq, L3_ffn_wk, L3_ffn_wv, L3_ffn_wo, L3_ffn_router_w, L3_ffn_w1, L3_ffn_w2, L3_ffn_w3)
    return h

_drawn_inputs = setup_inputs


def setup_inputs(seed=0):
    import zlib

    import numpy as np

    out = dict(_drawn_inputs(seed))
    spreads = {'L0_tok_b1': (0.0, 0.1),
     'L0_tok_gamma': (1.0, 0.2),
     'L0_tok_beta': (0.0, 0.1),
     'L0_tok_b2': (0.0, 0.1),
     'L0_ffn_gate_b': (0.0, 0.345),
     'L0_ffn_b1': (0.0, 0.8),
     'L0_ffn_b2': (0.0, 0.309),
     'L0_ffn_gamma': (1.0, 0.2),
     'L0_ffn_beta': (0.0, 0.1),
     'L1_ffn_b_gat': (0.0, 0.307),
     'L1_ffn_ln_gamma': (1.0, 0.6),
     'L1_ffn_ln_beta': (0.0, 0.8),
     'L1_ffn_b1': (0.0, 0.8),
     'L1_ffn_b2': (0.0, 0.29),
     'L2_attn_b_qkv': (0.0, 0.8),
     'L2_attn_kln_w': (1.0, 0.6),
     'L2_attn_kln_b': (0.0, 0.8),
     'L2_attn_vln_w': (1.0, 0.6),
     'L2_attn_vln_b': (0.0, 0.8),
     'L2_attn_b_proj': (0.0, 0.45),
     'L2_ffn_b1': (0.0, 0.637),
     'L2_ffn_b2': (0.0, 0.557),
     'L3_ffn_ln1_w': (1.0, 0.6),
     'L3_ffn_ln2_w': (1.0, 0.6)}
    factors = {'L0_ffn_w1': 8.0,
     'L0_ffn_w2': 8.0,
     'L1_attn_Wq': 2.809,
     'L1_attn_Wk': 2.887,
     'L1_ffn_W_gat': 8.0,
     'L1_ffn_att_src': 8.0,
     'L1_ffn_att_dst': 8.0,
     'L2_attn_W_qkv': 8.0,
     'L3_attn_Q': 2.889,
     'L3_attn_K': 3.088,
     'L3_ffn_wq': 8.0,
     'L3_ffn_wk': 8.0,
     'L3_ffn_wv': 8.0,
     'L3_ffn_wo': 8.0,
     'L3_ffn_router_w': 8.0,
     'L3_ffn_w1': 8.0,
     'L3_ffn_w2': 8.0,
     'L3_ffn_w3': 8.0}
    for name, (base, spread) in spreads.items():
        noise = np.random.default_rng([zlib.crc32(name.encode()), seed]).standard_normal(out[name].shape)
        drawn = base * np.exp(spread * noise) if base else spread * noise
        out[name] = jnp.asarray(drawn.astype(out[name].dtype))
    for name, factor in factors.items():
        out[name] = (out[name] * factor).astype(out[name].dtype)
    return out
```

```python
from contextlib import ExitStack, contextmanager
import numpy as np
import concourse.bass as bass
from concourse import mybir

F32 = mybir.dt.float32
BF16 = mybir.dt.bfloat16
I32 = mybir.dt.int32
U8 = mybir.dt.uint8
U32 = mybir.dt.uint32
ALU = mybir.AluOpType
ACT = mybir.ActivationFunctionType
AX = mybir.AxisListType

P = 128
B, S, D = 4, 512, 64
NT = B * S // P
TB = S // P
N = B * S
ATOMS = 100
LN_EPS = 1e-5
KD = 32
EDGES = 262144
NEG = -1e30


class Signal:

    def __init__(self, ctx, nc, name):
        self.sem = ctx.enter_context(nc.semaphore(name))
        self.count = 0


class Tally:

    def __init__(self, signal, start, per=0, i=0):
        self.s, self.start, self.per, self.i, self.k = signal, start, per, i, 0

    def up(self):
        self.k += 1
        return self.s.sem

    def at(self, k):
        return self.i * self.per + (self.start + k) if self.per else self.start + k


def bc(ap, axis, n):
    shape = list(ap.shape)
    shape.insert(axis, n)
    return ap.unsqueeze(axis).to_broadcast(shape)


CONSTS = {"ident": 128, "lower": 128, "causal": 128, "iota": 128, "col": 1, "heads": 64, "cos": 512, "sin": 512, "hi": 16}


def constants():
    out = np.zeros((P, sum(CONSTS.values())), np.float32)
    at = {}
    a = 0
    for n, w in CONSTS.items():
        at[n] = out[:, a:a + w]
        a += w
    r = np.arange(P)
    at["ident"][:] = np.eye(P)
    at["lower"][:] = r[:, None] <= r[None, :]
    at["causal"][:] = np.where(r[None, :] <= r[:, None], 0.0, NEG)
    at["iota"][:] = r[None, :]
    at["hi"][:] = np.arange(16)[None, :]
    at["col"][:, 0] = r
    at["heads"][:64] = (r[:64, None] // 4 == r[None, :64] // 4) / float(S)
    HD = 16
    inv = 1.0 / 10000.0 ** (np.arange(0, HD, 2, dtype=np.float32) / HD)
    freqs = np.outer(np.arange(S, dtype=np.float32), inv)
    emb = np.concatenate([freqs, freqs], axis=-1)
    for h in range(4):
        at["cos"][KD * h:KD * h + HD] = np.cos(emb).T
        at["sin"][KD * h:KD * h + HD] = np.sin(emb).T
        at["sin"][KD * h:KD * h + HD // 2] *= -1
    return out


def program(nc, T, out):
    with ExitStack() as ctx:
        _program(nc, T, out, ctx)


def _program(nc, T, out, ctx):
    def sb(name, shape, dt=F32):
        return ctx.enter_context(nc.sbuf_tensor(name, shape, dt))

    tensor_done = Signal(ctx, nc, "tensor_done")
    scalar_done = Signal(ctx, nc, "scalar_done")
    vector_done = Signal(ctx, nc, "vector_done")
    pool_done = Signal(ctx, nc, "pool_done")
    loaded = Signal(ctx, nc, "loaded")
    written = Signal(ctx, nc, "written")
    PS = ctx.enter_context(nc.psum_tensor("PS", [P, 8, 512], F32))
    PSh = PS[:].rearrange("p b n -> p (b n)").bitcast(BF16).rearrange("p (b n) -> p b n", b=8)

    @contextmanager
    def stage(pe=0, act=0, dve=0, pool=0, trips=1):
        per = lambda n: n if trips > 1 else 0
        marks = [(tensor_done, pe), (scalar_done, act), (vector_done, dve), (pool_done, pool)]
        with nc.Block() as block:
            made = []

            def tally(signal, n, i=0):
                t = Tally(signal, signal.count, per(n), i)
                made.append((t, n))
                return t

            def tallies(i=0):
                return [tally(s, n, i) for s, n in marks]

            yield block, tallies
        for s, n in marks:
            assert any(t.k for t, _ in made if t.s is s) == bool(n), s.sem
            for t, _ in made:
                assert t.s is not s or t.k in (0, n), (s.sem.name, t.k, n)
            s.count += n * trips

    H = sb("H", [P, NT, D])
    X = sb("X", [P, NT, D])
    XT = sb("XT", [D, N])
    tA = sb("tA", [P, NT, D])
    tB = sb("tB", [P, NT, D])
    st = sb("st", [P, 4, NT])
    Cc = sb("Cc", [P, sum(CONSTS.values())])
    C, a = {}, 0
    for n, w in CONSTS.items():
        C[n] = Cc[:, a:a + w]
        a += w
    W = {}
    for n, t in T.items():
        if n.startswith("w_"):
            W[n] = sb(n[2:] + "_sb", list(t.shape))
        if n.startswith("r_"):
            W[n] = sb(n[2:] + "_sb", [P] + list(t.shape))
    ident = C["ident"]

    def flat(t):
        return t[:].rearrange("p a b -> p (a b)")

    def transposed(src, dst, width=D):
        with stage(pe=NT, act=4) as (block, tallies):
            @block.tensor
            def _(eng):
                pe, _, _, _ = tallies()
                for t in range(NT):
                    nc.tensor.transpose(PS[0:width, t // 4, (t % 4) * P:(t % 4 + 1) * P], src[:, t, :], ident).then_inc(pe.up(), 1)

            @block.scalar
            def _(eng):
                pe, act, _, _ = tallies()
                for c in range(4):
                    eng.wait_ge(tensor_done.sem, pe.at(4 * c + 4))
                    nc.scalar.copy(dst[:, c * 512:(c + 1) * 512], PS[0:width, c, :]).then_inc(act.up(), 1)

    def normalised(src, dst, eps=LN_EPS, center=True, gamma=None, beta=None, turned=None, act_fn=None, eps_out=None):
        n = 5 + 3 * center + (gamma is not None) + (beta is not None)
        with stage(act=1 + (act_fn is not None), dve=n - 0) as (block, tallies):
            @block.vector
            def _(eng):
                _, act, dve, _ = tallies()

                def step(ins):
                    ins.then_inc(dve.up(), 1)
                    eng.wait_ge(vector_done.sem, dve.at(dve.k))

                v = nc.vector
                x = src[:]
                if center:
                    step(v.reduce_sum(st[:, 0, :], x, axis=AX.X))
                    step(v.tensor_scalar(st[:, 1, :], st[:, 0, :], 1.0 / D, None, ALU.mult))
                    step(v.tensor_tensor(tA[:], x, bc(st[:, 1, :], 2, D), ALU.subtract))
                    x = tA[:]
                step(v.tensor_tensor(tB[:], x, x, ALU.mult))
                step(v.reduce_sum(st[:, 2, :], tB[:], axis=AX.X))
                step(v.tensor_scalar(st[:, 2, :], st[:, 2, :], 1.0 / D, eps, ALU.mult, ALU.add))
                eng.wait_ge(scalar_done.sem, act.at(1))
                step(v.reciprocal(st[:, 3, :], st[:, 3, :]))
                step(v.tensor_tensor(dst[:], x, bc(st[:, 3, :], 2, D), ALU.mult))
                if gamma is not None:
                    step(v.tensor_tensor(dst[:], dst[:], bc(gamma, 1, NT), ALU.mult))
                if beta is not None:
                    step(v.tensor_tensor(dst[:], dst[:], bc(beta, 1, NT), ALU.add))

            @block.scalar
            def _(eng):
                _, act, dve, _ = tallies()
                eng.wait_ge(vector_done.sem, dve.at(3 + 3 * center))
                nc.scalar.activation(st[:, 3, :], st[:, 2, :], ACT.Sqrt).then_inc(act.up(), 1)
                if act_fn is not None:
                    eng.wait_ge(vector_done.sem, dve.at(n))
                    nc.scalar.activation(dst[:], dst[:], act_fn).then_inc(act.up(), 1)
        if turned is not None:
            transposed(dst, turned)

    def projected(srcs, width, dst, bias=None, add=None):
        per_bank = 8
        nb = NT // per_bank
        with stage(pe=NT, dve=nb) as (block, tallies):
            @block.tensor
            def _(eng):
                pe, _, _, _ = tallies()
                for t in range(NT):
                    o = PS[:, t // per_bank, (t % per_bank) * width:(t % per_bank + 1) * width]
                    for j, (s, w) in enumerate(srcs):
                        ins = nc.tensor.matmul(o, s[:, t * P:(t + 1) * P], w(t) if callable(w) else w, start=(j == 0), stop=(j == len(srcs) - 1))
                    ins.then_inc(pe.up(), 1)

            @block.vector
            def _(eng):
                pe, _, dve, _ = tallies()
                for c in range(nb):
                    tiles = slice(c * per_bank, (c + 1) * per_bank)
                    eng.wait_ge(tensor_done.sem, pe.at((c + 1) * per_bank))
                    p = PS[:, c, 0:per_bank * width].rearrange("p (t n) -> p t n", n=width)
                    if add is not None:
                        nc.vector.tensor_tensor(dst[:, tiles, :], p, add[:, tiles, :], ALU.add).then_inc(dve.up(), 1)
                    elif bias is not None:
                        nc.vector.tensor_tensor(dst[:, tiles, :], p, bc(bias, 1, per_bank), ALU.add).then_inc(dve.up(), 1)
                    else:
                        nc.vector.tensor_copy(dst[:, tiles, :], p).then_inc(dve.up(), 1)

    def summed(dst, x, y):
        with stage(dve=1) as (block, tallies):
            @block.vector
            def _(eng):
                _, _, dve, _ = tallies()
                nc.vector.tensor_tensor(dst[:], x[:], y[:], ALU.add).then_inc(dve.up(), 1)

    arena = sb("arena", [P, 15360])

    def part(at, shape, dt=F32, rows=P):
        words = int(np.prod(shape)) * (1 if dt == U8 else 4) // 4
        v = arena[0:rows, at:at + words]
        if dt != F32:
            v = v.bitcast(dt)
        names = "abcdef"[:len(shape)]
        if len(shape) > 1:
            v = v.rearrange(f"p ({' '.join(names)}) -> p {' '.join(names)}", **{n: k for n, k in zip(names, shape)})
        return v

    XTb = sb("XTb", [D, S])
    QTb = part(0, [2, S])
    KTb = part(1024, [2, S])
    Eb = part(2048, [2, S])
    Pb = part(3072, [2, S])
    PTb = part(4096, [2, S])
    AT = part(5120, [2, TB, S])
    Vb = part(9216, [TB, 8, D + 1])
    mraw = sb("mraw", [P, 2, 1])
    nmax = sb("nmax", [P, 2, 1])
    rden = sb("rden", [P, 2, TB])
    oacc = sb("oacc", [P, 2, TB, D])

    def softmax_attention(heads, rows, wq, wk, wv, dst, scale, ones=1.0, causal=False, rope=None):
        per_group = min(heads, P // rows)
        groups = heads // per_group
        width = P
        units = [(q, h) for q in range(TB) for h in range(heads)]
        U = len(units)
        NV = heads * D
        rp = 2 if rope else 1
        PE = 2 * groups * rp + TB + 3 * U
        AC = 1 + (0 if rope else 2 * groups) + TB + 2 * U
        ones_k = 1
        DV = ones_k + (6 * groups if rope else 0) + (4 + causal) * U
        with stage(pe=PE, act=AC, dve=DV, trips=B) as (block, tallies):
            proj_pe = 2 * groups * rp + TB
            proj_act = 1 + (0 if rope else 2 * groups) + TB
            proj_dve = ones_k + (6 * groups if rope else 0)

            def keys(q):
                return (q + 1) * P if causal else S

            def order(steps):
                at, k = {}, 0
                for s in range(U + 2):
                    for name, lag in steps:
                        if 0 <= s - lag < U:
                            k += steps[(name, lag)]
                            at[(name, s - lag)] = k
                return at

            pe_at = order({("s", 0): 1, ("t", 1): 1, ("m", 2): 1})
            act_at = order({("e", 0): 1, ("c", 1): 1})
            dve_at = order({("x", 0): 2 + causal, ("n", 2): 2})

            def act_exp(u):
                return proj_act + act_at[("e", u)]

            def act_copy(u):
                return proj_act + act_at[("c", u)]

            def dve_max(u):
                return proj_dve + dve_at[("x", u)]

            def dve_norm(u):
                return proj_dve + dve_at[("n", u)]

            def pe_of(name, u):
                return proj_pe + pe_at[(name, u)]

            @block.tensor
            def _(eng):
                with eng.Fori(0, B) as i:
                    pe, act, dve, _ = tallies(i)
                    eng.wait_ge(scalar_done.sem, act.at(1))
                    eng.wait_ge(vector_done.sem, dve.at(0))
                    for n, w in enumerate([x for g in range(groups) for x in (wq[g], wk[g])]):
                        for r in range(rp):
                            nc.tensor.matmul(PS[0:width, n * rp + r, :], w[r] if rope else w, XTb[:], start=True, stop=True).then_inc(pe.up(), 1)
                    for t in range(TB):
                        nc.tensor.matmul(PS[:, 4 + t, 0:NV], XTb[:, t * P:(t + 1) * P], wv, start=True, stop=True).then_inc(pe.up(), 1)
                    eng.wait_ge(scalar_done.sem, act.at(proj_act))
                    eng.wait_ge(vector_done.sem, dve.at(proj_dve))

                    def scores(u):
                        q, h = units[u]
                        g, r = divmod(h, per_group)
                        if u >= 2:
                            eng.wait_ge(scalar_done.sem, act.at(act_exp(u - 2)))
                        rr = slice(r * rows, (r + 1) * rows)
                        nc.tensor.matmul(PS[:, u % 2, 0:keys(q)], QTb[rr, g, q * P:(q + 1) * P], KTb[rr, g, 0:keys(q)], start=True, stop=True).then_inc(pe.up(), 1)

                    def turn(u):
                        q, h = units[u]
                        eng.wait_ge(scalar_done.sem, act.at(act_exp(u)))
                        n = keys(q) // P
                        for k in range(n):
                            ins = nc.tensor.transpose(PS[:, 2 + u % 2, k * P:(k + 1) * P], Pb[:, u % 2, k * P:(k + 1) * P], ident)
                        ins.then_inc(pe.up(), 1)

                    def mix(u):
                        q, h = units[u]
                        eng.wait_ge(scalar_done.sem, act.at(act_copy(u)))
                        if u >= 2:
                            eng.wait_ge(vector_done.sem, dve.at(dve_norm(u - 2)))
                        n = keys(q) // P
                        for k in range(n):
                            ins = nc.tensor.matmul(PS[:, 4 + u % 2, 0:D + 1], PTb[:, u % 2, k * P:(k + 1) * P], Vb[:, k, h, :], start=(k == 0), stop=(k == n - 1))
                        ins.then_inc(pe.up(), 1)

                    for s in range(U + 2):
                        if s < U:
                            scores(s)
                        if 1 <= s <= U:
                            turn(s - 1)
                        if s >= 2:
                            mix(s - 2)

            @block.scalar
            def _(eng):
                with eng.Fori(0, B) as i:
                    pe, act, dve, _ = tallies(i)
                    eng.wait_ge(tensor_done.sem, pe.at(0))
                    nc.scalar.copy(XTb[:], XT[:, bass.ds(i * S, S)]).then_inc(act.up(), 1)
                    if not rope:
                        for n in range(2 * groups):
                            eng.wait_ge(tensor_done.sem, pe.at(n + 1))
                            nc.scalar.copy((KTb if n % 2 else QTb)[0:width, n // 2, :], PS[0:width, n, :]).then_inc(act.up(), 1)
                    for t in range(TB):
                        eng.wait_ge(tensor_done.sem, pe.at(2 * groups * rp + t + 1))
                        nc.scalar.copy(Vb[:, t, 0:heads, 0:D], PS[:, 4 + t, 0:NV].rearrange("p (h d) -> p h d", d=D)).then_inc(act.up(), 1)
                    for s in range(U + 2):
                        if s < U:
                            q, h = units[s]
                            eng.wait_ge(vector_done.sem, dve.at(dve_max(s)))
                            if s >= 2:
                                eng.wait_ge(tensor_done.sem, pe.at(pe_of("t", s - 2)))
                            nc.scalar.activation(Pb[:, s % 2, 0:keys(q)], PS[:, s % 2, 0:keys(q)], ACT.Exp, bias=nmax[:, s % 2, :], scale=scale).then_inc(act.up(), 1)
                        if 1 <= s <= U:
                            u = s - 1
                            q, h = units[u]
                            eng.wait_ge(tensor_done.sem, pe.at(pe_of("t", u)))
                            if u >= 2:
                                eng.wait_ge(tensor_done.sem, pe.at(pe_of("m", u - 2)))
                            nc.scalar.copy(PTb[:, u % 2, 0:keys(q)], PS[:, 2 + u % 2, 0:keys(q)]).then_inc(act.up(), 1)

            @block.vector
            def _(eng):
                with eng.Fori(0, B) as i:
                    pe, act, dve, _ = tallies(i)
                    eng.wait_ge(tensor_done.sem, pe.at(0))
                    nc.vector.memset(Vb[:, :, 0:heads, D:D + 1], ones).then_inc(dve.up(), 1)
                    if rope:
                        for g in range(groups):
                            for n, dstb in ((0, QTb), (1, KTb)):
                                bank = (2 * g + n) * 2
                                eng.wait_ge(tensor_done.sem, pe.at(bank + 2))
                                nc.vector.tensor_tensor(dstb[:, g, :], PS[:, bank, :], rope[0], ALU.mult).then_inc(dve.up(), 1)
                                nc.vector.tensor_tensor(Eb[:, n, :], PS[:, bank + 1, :], rope[1], ALU.mult).then_inc(dve.up(), 1)
                                eng.wait_ge(vector_done.sem, dve.at(dve.k))
                                nc.vector.tensor_tensor(dstb[:, g, :], dstb[:, g, :], Eb[:, n, :], ALU.add).then_inc(dve.up(), 1)
                    for s in range(U + 2):
                        if s < U:
                            q, h = units[s]
                            eng.wait_ge(tensor_done.sem, pe.at(pe_of("s", s)))
                            if s >= 2:
                                eng.wait_ge(scalar_done.sem, act.at(act_exp(s - 2)))
                            if causal:
                                diag = PS[:, s % 2, q * P:(q + 1) * P]
                                nc.vector.tensor_tensor(diag, diag, C["causal"], ALU.add).then_inc(dve.up(), 1)
                                eng.wait_ge(vector_done.sem, dve.at(dve.k))
                            nc.vector.reduce_max(mraw[:, s % 2, :], PS[:, s % 2, 0:keys(q)], axis=AX.X).then_inc(dve.up(), 1)
                            eng.wait_ge(vector_done.sem, dve.at(dve.k))
                            nc.vector.tensor_scalar(nmax[:, s % 2, :], mraw[:, s % 2, :], -scale, None, ALU.mult).then_inc(dve.up(), 1)
                        if s >= 2:
                            u = s - 2
                            q, h = units[u]
                            o = PS[:, 4 + u % 2, :]
                            eng.wait_ge(tensor_done.sem, pe.at(pe_of("m", u)))
                            nc.vector.reciprocal(rden[:, u % 2, 0:1], o[:, D:D + 1]).then_inc(dve.up(), 1)
                            eng.wait_ge(vector_done.sem, dve.at(dve.k))
                            y = dst[:, bass.ds(i * TB + q, 1), :].rearrange("p a d -> p (a d)")
                            nc.vector.scalar_tensor_tensor(out=y, in0=o[:, 0:D], scalar=rden[:, u % 2, 0:1], in1=y, op0=ALU.mult, op1=ALU.add).then_inc(dve.up(), 1)

    def linear_attention(heads, wq, wk, wv, dst, eps):
        groups = heads // 4
        NV = heads * D
        NP_ = 2 * groups
        proj_pe = NP_ + TB
        PE = proj_pe + 2 * heads
        proj_act = 1 + NP_ + TB
        AC = proj_act + heads
        proj_dve = 1 + 2 * NP_
        DV = proj_dve + 5 * heads
        with stage(pe=PE, act=AC, dve=DV, trips=B) as (block, tallies):
            def dve_mask(h):
                return h + 1 + 4 * max(0, h - 1)

            def dve_norm(h):
                return min(h + 2, heads) + 4 * (h + 1)

            def pe_scores(h):
                return proj_pe + (1 if h == 0 else 2 * h)

            def pe_mix(h):
                return proj_pe + (2 * h + 3 if h + 1 < heads else 2 * heads)

            @block.tensor
            def _(eng):
                with eng.Fori(0, B) as i:
                    pe, act, dve, _ = tallies(i)
                    eng.wait_ge(scalar_done.sem, act.at(1))
                    eng.wait_ge(vector_done.sem, dve.at(0))
                    for n, w in enumerate([x for g in range(groups) for x in (wq[g], wk[g])]):
                        nc.tensor.matmul(PS[:, n, :], w, XTb[:], start=True, stop=True).then_inc(pe.up(), 1)
                    for t in range(TB):
                        nc.tensor.matmul(PS[:, 4 + t, 0:NV], XTb[:, t * P:(t + 1) * P], wv, start=True, stop=True).then_inc(pe.up(), 1)
                    eng.wait_ge(scalar_done.sem, act.at(proj_act))
                    eng.wait_ge(vector_done.sem, dve.at(proj_dve))

                    def scores(h):
                        g, r = divmod(h, 4)
                        rr = slice(r * KD, (r + 1) * KD)
                        if h >= 1:
                            eng.wait_ge(scalar_done.sem, act.at(proj_act + h))
                        for k in range(TB):
                            ins = nc.tensor.matmul(PS[:, k, k * P:S], KTb[rr, g, k * P:(k + 1) * P], QTb[rr, g, k * P:S], start=True, stop=True)
                        ins.then_inc(pe.up(), 1)

                    def mix(h):
                        eng.wait_ge(scalar_done.sem, act.at(proj_act + h + 1))
                        eng.wait_ge(vector_done.sem, dve.at(proj_dve + dve_mask(h)))
                        if h >= 2:
                            eng.wait_ge(vector_done.sem, dve.at(proj_dve + dve_norm(h - 2)))
                        for q in range(TB):
                            for k in range(q + 1):
                                ins = nc.tensor.matmul(PS[:, 4 + h % 2, q * (D + 1):(q + 1) * (D + 1)], AT[:, h % 2, k, q * P:(q + 1) * P], Vb[:, k, h, :], start=(k == 0), stop=(k == q))
                        ins.then_inc(pe.up(), 1)

                    scores(0)
                    for h in range(heads):
                        if h + 1 < heads:
                            scores(h + 1)
                        mix(h)

            @block.scalar
            def _(eng):
                with eng.Fori(0, B) as i:
                    pe, act, dve, _ = tallies(i)
                    eng.wait_ge(tensor_done.sem, pe.at(0))
                    nc.scalar.copy(XTb[:], XT[:, bass.ds(i * S, S)]).then_inc(act.up(), 1)
                    for n in range(NP_):
                        eng.wait_ge(vector_done.sem, dve.at(1 + n + 1 + max(0, n - 1)))
                        nc.scalar.activation(Eb[:, n % 2, :], Eb[:, n % 2, :], ACT.Exp).then_inc(act.up(), 1)
                    for t in range(TB):
                        eng.wait_ge(tensor_done.sem, pe.at(NP_ + t + 1))
                        nc.scalar.copy(Vb[:, t, 0:heads, 0:D], PS[:, 4 + t, 0:NV].rearrange("p (h d) -> p h d", d=D)).then_inc(act.up(), 1)
                    for h in range(heads):
                        eng.wait_ge(tensor_done.sem, pe.at(pe_scores(h)))
                        if h >= 2:
                            eng.wait_ge(tensor_done.sem, pe.at(pe_mix(h - 2)))
                            eng.wait_ge(vector_done.sem, dve.at(proj_dve + dve_mask(h - 2)))
                        for k in range(TB):
                            ins = nc.scalar.copy(AT[:, h % 2, k, k * P:S], PS[:, k, k * P:S])
                        ins.then_inc(act.up(), 1)

            @block.vector
            def _(eng):
                with eng.Fori(0, B) as i:
                    pe, act, dve, _ = tallies(i)
                    eng.wait_ge(tensor_done.sem, pe.at(0))
                    nc.vector.memset(Vb[:, :, 0:heads, D:D + 1], 1.0).then_inc(dve.up(), 1)
                    for n in range(NP_ + 1):
                        if n < NP_:
                            eng.wait_ge(tensor_done.sem, pe.at(n + 1))
                            if n >= 2:
                                eng.wait_ge(vector_done.sem, dve.at(dve.k))
                            nc.vector.tensor_scalar(Eb[:, n % 2, :], PS[:, n, :], 0.0, None, ALU.min).then_inc(dve.up(), 1)
                        if n >= 1:
                            m = n - 1
                            eng.wait_ge(scalar_done.sem, act.at(1 + n))
                            dstb = (KTb if m % 2 else QTb)[:, m // 2, :]
                            nc.vector.scalar_tensor_tensor(out=dstb, in0=PS[:, m, :], scalar=0.0, in1=Eb[:, m % 2, :], op0=ALU.max, op1=ALU.add).then_inc(dve.up(), 1)

                    def mask(h):
                        eng.wait_ge(scalar_done.sem, act.at(proj_act + h + 1))
                        for k in range(TB):
                            kk = AT[:, h % 2, k, k * P:(k + 1) * P]
                            ins = nc.vector.tensor_tensor(kk, kk, C["lower"], ALU.mult)
                        ins.then_inc(dve.up(), 1)

                    def step(ins):
                        ins.then_inc(dve.up(), 1)
                        eng.wait_ge(vector_done.sem, dve.at(dve.k))

                    mask(0)
                    for h in range(heads):
                        if h + 1 < heads:
                            mask(h + 1)
                        o = PS[:, 4 + h % 2, 0:TB * (D + 1)].rearrange("p (q n) -> p q n", n=D + 1)
                        eng.wait_ge(tensor_done.sem, pe.at(pe_mix(h)))
                        step(nc.vector.tensor_scalar(rden[:, h % 2, :], o[:, :, D:D + 1].rearrange("p q a -> p (q a)"), eps, None, ALU.add))
                        step(nc.vector.reciprocal(rden[:, h % 2, :], rden[:, h % 2, :]))
                        step(nc.vector.tensor_tensor(oacc[:, h % 2, :, :], o[:, :, 0:D], bc(rden[:, h % 2, :], 2, D), ALU.mult))
                        y = dst[:, bass.ds(i * TB, TB), :]
                        step(nc.vector.tensor_tensor(y, y, oacc[:, h % 2, :, :], ALU.add))

    def weight_products(pairs, dst, split):
        with stage(pe=1, act=1) as (block, tallies):
            @block.tensor
            def _(eng):
                pe, _, _, _ = tallies()
                for n, (l, r) in enumerate(pairs):
                    ins = nc.tensor.matmul(PS[0:D, 0, n * D:(n + 1) * D], l, r, start=True, stop=True)
                ins.then_inc(pe.up(), 1)

            @block.scalar
            def _(eng):
                pe, act, _, _ = tallies()
                eng.wait_ge(tensor_done.sem, pe.at(1))
                nc.scalar.copy(dst[:, 0:len(pairs) * D], PS[0:D, 0, 0:len(pairs) * D]).then_inc(act.up(), 1)

    L16 = sb("L16", [P, NT, 16])
    G16 = sb("G16", [P, NT, 16])
    M16 = sb("M16", [P, NT, 16])
    top = sb("top", [P, NT, 8])
    pos = sb("pos", [P, NT, 8], U32)
    posf = sb("posf", [P, NT, 2])
    g2 = sb("g2", [P, 4, NT])
    GT = sb("GT", [16, N])
    HT = sb("HT", [P, 2, 2, S])

    def top2_gates(E, eps=None):
        W_ = max(E, 8)
        n = (E < 8) + 2 * NT + 1 + 1 + 1 + 1 + 1 + 5 + (3 if eps is not None else 0)
        with stage(act=1 + (eps is not None), dve=n) as (block, tallies):
            @block.vector
            def _(eng):
                _, act, dve, _ = tallies()
                v = nc.vector

                def step(ins):
                    ins.then_inc(dve.up(), 1)
                    eng.wait_ge(vector_done.sem, dve.at(dve.k))

                if E < 8:
                    step(v.memset(L16[:, :, E:8], -3.0e38))
                for t in range(NT):
                    v.max(top[:, t, :], L16[:, t, 0:W_]).then_inc(dve.up(), 1)
                eng.wait_ge(vector_done.sem, dve.at(dve.k))
                for t in range(NT):
                    v.max_index(pos[:, t, :], top[:, t, :], L16[:, t, 0:W_]).then_inc(dve.up(), 1)
                step(v.tensor_tensor(g2[:, 0, :], top[:, :, 1], top[:, :, 0], ALU.subtract))
                step(v.tensor_copy(posf[:], pos[:, :, 0:2]))
                k0 = dve.k
                if eps is not None:
                    step(v.tensor_tensor(M16[:, :, 0:E], L16[:, :, 0:E], bc(top[:, :, 0], 2, E), ALU.subtract))
                eng.wait_ge(scalar_done.sem, act.at(1))
                if eps is not None:
                    eng.wait_ge(scalar_done.sem, act.at(2))
                    step(v.reduce_sum(g2[:, 3, :], M16[:, :, 0:E], axis=AX.X))
                    step(v.scalar_tensor_tensor(out=g2[:, 2, :], in0=g2[:, 3, :], scalar=eps, in1=g2[:, 1, :], op0=ALU.mult, op1=ALU.add))
                    step(v.tensor_scalar(g2[:, 2, :], g2[:, 2, :], 1.0, None, ALU.add))
                else:
                    step(v.tensor_scalar(g2[:, 2, :], g2[:, 1, :], 1.0, None, ALU.add))
                step(v.reciprocal(g2[:, 2, :], g2[:, 2, :]))
                step(v.tensor_tensor(g2[:, 3, :], g2[:, 1, :], g2[:, 2, :], ALU.mult))
                step(v.tensor_tensor(G16[:, :, 0:E], bc(C["hi"][:, 0:E], 1, NT), bc(posf[:, :, 0], 2, E), ALU.is_equal))
                step(v.tensor_tensor(M16[:, :, 0:E], bc(C["hi"][:, 0:E], 1, NT), bc(posf[:, :, 1], 2, E), ALU.is_equal))
                step(v.tensor_tensor(G16[:, :, 0:E], G16[:, :, 0:E], bc(g2[:, 2, :], 2, E), ALU.mult))
                step(v.tensor_tensor(M16[:, :, 0:E], M16[:, :, 0:E], bc(g2[:, 3, :], 2, E), ALU.mult))
                step(v.tensor_tensor(G16[:, :, 0:E], G16[:, :, 0:E], M16[:, :, 0:E], ALU.add))
                assert dve.k == n, (dve.k, n)

            @block.scalar
            def _(eng):
                _, act, dve, _ = tallies()
                k = (E < 8) + 2 * NT + 1
                eng.wait_ge(vector_done.sem, dve.at(k))
                nc.scalar.activation(g2[:, 1, :], g2[:, 0, :], ACT.Exp).then_inc(act.up(), 1)
                if eps is not None:
                    eng.wait_ge(vector_done.sem, dve.at(k + 2))
                    nc.scalar.activation(M16[:, :, 0:E], M16[:, :, 0:E], ACT.Exp).then_inc(act.up(), 1)

    def experts(E, parts, w1, w2, act_fn, acc, b1=None, w3=None, share=1):
        F = len(parts)
        up = 2 if w3 else 1
        G = E // share
        units = [(g, f) for g in range(G) for f in range(F)]
        U = len(units)
        PE = U * up + G
        AC = 1 + U
        DV = (U if w3 else 0) + 2 * E

        def ends(s):
            return 2 <= s and (s - 2) % F == F - 1

        with stage(pe=PE, act=AC, dve=DV, trips=B) as (block, tallies):
            pe_up, pe_down, dve_mul, dve_acc, kp, kd = {}, {}, {}, {}, 0, 0
            for s in range(U + 2):
                if s < U:
                    kp += up
                    pe_up[s] = kp
                if 1 <= s <= U and w3:
                    kd += 1
                    dve_mul[s - 1] = kd
                if ends(s):
                    g = (s - 2) // F
                    kp += 1
                    pe_down[g] = kp
                    kd += 2 * share
                    dve_acc[g] = kd

            @block.tensor
            def _(eng):
                with eng.Fori(0, B) as i:
                    pe, act, dve, _ = tallies(i)
                    eng.wait_ge(scalar_done.sem, act.at(1))
                    eng.wait_ge(vector_done.sem, dve.at(0))
                    for s in range(U + 2):
                        if s < U:
                            g, f = units[s]
                            if s >= 2:
                                if w3:
                                    eng.wait_ge(vector_done.sem, dve.at(dve_mul[s - 2]))
                                eng.wait_ge(scalar_done.sem, act.at(1 + s - 1))
                            nc.tensor.matmul(PS[0:parts[f], s % 2, :], w1(g, f), XTb[:], start=True, stop=True).then_inc(pe.up(), 1)
                            if w3:
                                nc.tensor.matmul(PS[0:parts[f], 2 + s % 2, :], w3(g, f), XTb[:], start=True, stop=True).then_inc(pe.up(), 1)
                        if ends(s):
                            g = (s - 2) // F
                            if w3:
                                eng.wait_ge(vector_done.sem, dve.at(dve_mul[s - 2]))
                            else:
                                eng.wait_ge(scalar_done.sem, act.at(1 + s - 1))
                            if g >= 2:
                                eng.wait_ge(vector_done.sem, dve.at(dve_acc[g - 2]))
                            for j in range(share):
                                for t in range(TB):
                                    for f in range(F):
                                        n = parts[f] // share
                                        o = t * D
                                        ins = nc.tensor.matmul(PS[:, 4 + 2 * (g % 2) + j, o:o + D], HT[j * n:(j + 1) * n, g % 2, f, t * P:(t + 1) * P], w2(g, j, f), start=(f == 0), stop=(f == F - 1))
                            ins.then_inc(pe.up(), 1)

            @block.scalar
            def _(eng):
                with eng.Fori(0, B) as i:
                    pe, act, dve, _ = tallies(i)
                    eng.wait_ge(tensor_done.sem, pe.at(0))
                    nc.scalar.copy(XTb[:], XT[:, bass.ds(i * S, S)]).then_inc(act.up(), 1)
                    for s in range(U):
                        g, f = units[s]
                        eng.wait_ge(tensor_done.sem, pe.at(pe_up[s]))
                        if g >= 2:
                            eng.wait_ge(tensor_done.sem, pe.at(pe_down[g - 2]))
                        bias = b1(g, f) if b1 else 0.0
                        nc.scalar.activation(HT[0:parts[f], g % 2, f, :], PS[0:parts[f], s % 2, :], act_fn, bias=bias).then_inc(act.up(), 1)

            @block.vector
            def _(eng):
                with eng.Fori(0, B) as i:
                    pe, act, dve, _ = tallies(i)
                    for s in range(U + 2):
                        if 1 <= s <= U and w3:
                            g, f = units[s - 1]
                            eng.wait_ge(scalar_done.sem, act.at(1 + s))
                            h = HT[0:parts[f], g % 2, f, :]
                            nc.vector.tensor_tensor(h, h, PS[0:parts[f], 2 + (s - 1) % 2, :], ALU.mult).then_inc(dve.up(), 1)
                        if ends(s):
                            g = (s - 2) // F
                            eng.wait_ge(tensor_done.sem, pe.at(pe_down[g]))
                            for j in range(share):
                                e = g * share + j
                                gate = G16[:, bass.ds(i * TB, TB), e:e + 1].to_broadcast([P, TB, D])
                                o = PS[:, 4 + 2 * (g % 2) + j, 0:TB * D].rearrange("p (t d) -> p t d", d=D)
                                nc.vector.tensor_tensor(oacc[:, e % 2, :, :], o, gate, ALU.mult).then_inc(dve.up(), 1)
                                eng.wait_ge(vector_done.sem, dve.at(dve.k))
                                y = acc[:, bass.ds(i * TB, TB), :]
                                nc.vector.tensor_tensor(y, y, oacc[:, e % 2, :, :], ALU.add).then_inc(dve.up(), 1)
                                eng.wait_ge(vector_done.sem, dve.at(dve.k))

    def features(w, srcs_T, dst, scale=None, bias=None):
        rows = dst.shape[0]
        with stage(pe=4, act=4) as (block, tallies):
            @block.tensor
            def _(eng):
                pe, _, _, _ = tallies()
                for c in range(4):
                    terms = w(c) if callable(w) else [(w, srcs_T[:, c * S:(c + 1) * S])]
                    for j, (l, r) in enumerate(terms):
                        ins = nc.tensor.matmul(PS[0:rows, c, :], l, r, start=(j == 0), stop=(j == len(terms) - 1))
                    ins.then_inc(pe.up(), 1)

            @block.scalar
            def _(eng):
                pe, act, _, _ = tallies()
                for c in range(4):
                    eng.wait_ge(tensor_done.sem, pe.at(c + 1))
                    nc.scalar.activation(dst[:, c * S:(c + 1) * S], PS[0:rows, c, :], ACT.Identity,
                                         bias=0.0 if bias is None else bias, scale=1.0 if scale is None else scale).then_inc(act.up(), 1)

    REL = part(0, [NT, S])
    ADJ = part(8192, [NT, S], U8)
    ADJ4 = part(8192, [NT, S // 4], I32)
    OH = part(10240, [N], rows=ATOMS)
    ids = part(12288, [N], I32, rows=ATOMS)
    NB = sb("NB", [P, NT, D])
    ET = sb("ET", [D, N])
    Y = sb("Y", [P, NT, D])
    R = sb("R", [P, NT, D])
    KVm = sb("KVm", [D, B, D])
    MV = sb("MV", [D, 8 * D])
    notident = sb("notident", [P, P])
    identh = sb("identh", [P, P], BF16)

    loads = [(Cc[:], T["consts"]), (ids[:], T["ids"].partition_broadcast(ATOMS)), (REL[:], T["rel"]), (ADJ4, T["adj"])]
    for n, w in W.items():
        loads.append((w[:], T[n] if n.startswith("w_") else T[n].partition_broadcast(P)))
    with stage() as (block, tallies):
        @block.sync
        def _(eng):
            for d, s in loads[::2]:
                eng.dma_start(d, s).then_inc(loaded.sem, 16)
            eng.wait_ge(loaded.sem, 16 * len(loads))

        @block.scalar
        def _(eng):
            for d, s in loads[1::2]:
                eng.dma_start(d, s).then_inc(loaded.sem, 16)

    w = lambda n: W["w_" + n][:]
    row = lambda n: W["r_" + n][:]

    with stage(dve=4 + TB) as (block, tallies):
        @block.vector
        def _(eng):
            _, _, dve, _ = tallies()
            nc.vector.tensor_copy(identh[:], ident).then_inc(dve.up(), 1)
            nc.vector.tensor_scalar(OH[:], ids[:], C["col"][0:ATOMS], None, ALU.is_equal).then_inc(dve.up(), 1)
            nc.vector.tensor_scalar(notident[:], ident, -1.0, 1.0, ALU.mult, ALU.add).then_inc(dve.up(), 1)
            nc.vector.scalar_tensor_tensor(out=REL[:], in0=ADJ[:], scalar=0.0, in1=REL[:], op0=ALU.not_equal, op1=ALU.mult).then_inc(dve.up(), 1)
            eng.wait_ge(vector_done.sem, dve.at(4))
            for j in range(TB):
                v = REL[:].rearrange("p (b j) i -> p b j i", b=B)[:, :, j, j * P:(j + 1) * P]
                nc.vector.tensor_tensor(v, v, bc(notident[:], 1, B), ALU.mult).then_inc(dve.up(), 1)
    features(w("atom_embed"), OH, ET[:])
    projected([(OH, w("neighbor_embed"))], D, NB)
    NF = XT
    features(lambda b: [(NB[:, b * TB + j, :], REL[:, b * TB + j, :]) for j in range(TB)], None, NF[:], scale=w("w_rd"))
    projected([(ET, w("tok_w1a")), (NF, w("tok_w1b"))], D, Y, bias=row("tok_b1"))
    normalised(Y, X, gamma=row("tok_gamma"), beta=row("tok_beta"), act_fn=ACT.Silu)
    transposed(X, XT)
    projected([(XT, w("tok_w2"))], D, H, bias=row("tok_b2"))

    def l0_attn():
        normalised(H, X, turned=XT)
        weight_products([(w("a0_wvT")[:, h * D:(h + 1) * D], w("a0_wo")[:, h * D:(h + 1) * D]) for h in range(8)], MV, D)
        q, k = w("a0_wq"), w("a0_wk")
        linear_attention(8, [q[:, 0:P], q[:, P:2 * P]], [k[:, 0:P], k[:, P:2 * P]], MV[:], H, 1e-9)

    def l0_ffn():
        normalised(H, X, turned=XT)
        projected([(XT, w("f0_gate"))], 16, L16, bias=row("f0_gate_b"))
        top2_gates(16)
        transposed(G16, GT[:], 16)
        projected([(GT, w("f0_b2"))], D, Y, add=X)
        experts(16, [P], lambda e, f: w("f0_w1")[:, e * P:(e + 1) * P], lambda e, j, f: w("f0_w2")[:, e * D:(e + 1) * D],
                ACT.Relu, Y, b1=lambda e, f: w("f0_b1")[:, e:e + 1])
        normalised(Y, X, gamma=row("f0_gamma"), beta=row("f0_beta"))
        summed(H, H, X)

    def l1_attn():
        normalised(H, X, turned=XT)
        softmax_attention(1, D, [w("a1_wq")], [w("a1_wk")], w("a1_wv"), H, 1.0, ones=float(D) ** 0.5)

    HALF = EDGES // P // 2
    BITS = HALF.bit_length() - 1
    COLS = HALF + 16
    C4 = 4
    HV, SV = 16, 20
    LAG = 4
    assert 2 ** BITS == HALF and 22 + BITS == 32
    edge_src = part(0, [2, HALF], I32)
    edge_dst = part(2048, [2, HALF], I32)
    packed = [part(4096, [2, HALF], I32), part(0, [2, HALF], I32)]
    moves = part(2048, [2, HALF], I32)
    stays = part(6144, [2, HALF], I32)
    outside = part(8192, [2, HALF])
    distance = part(10240, [2, HALF])
    column = part(12288, [HALF])
    srclo, srchi, dstlo, dsthi = (part(6144 + k * 2 * COLS, [2 * COLS]) for k in range(4))
    field = part(2048, [2, HALF], I32)
    OHs = part(0, [2, C4, P // 2]).bitcast(BF16)
    OHd = part(512, [4, C4, P])
    OHsT = part(2560, [2, C4, P // 2]).bitcast(BF16)
    OHdT = part(3072, [2, C4, P // 2]).bitcast(BF16)
    spread = part(3584, [2, C4, 16, SV])
    assert 3584 + 2 * C4 * 16 * SV <= 6144 and 6144 + 8 * COLS <= 15360
    pickS = tA[:].rearrange("p a b -> p (a b)").rearrange("p (c h v) -> p c h v", c=C4, h=16)
    tBf = tB[:].rearrange("p a b -> p (a b)")
    pickD = tBf[:, 0:256].rearrange("p (c h v) -> p c h v", c=C4, h=16)
    sm = [tBf[:, 256 + 16 * k:272 + 16 * k].rearrange("p (c h) -> p c h", c=C4) for k in range(6)]
    hatt = tBf[:, 384:448].rearrange("p (c v) -> p c v", c=C4)
    maskS = sb("maskS", [P, 2, C4, 16])
    maskD = sb("maskD", [P, 4, C4, 16])
    vals = sb("vals", [P, 2, C4, SV])
    tabS = sb("tabS", [P, 3, NT, HV], BF16)
    tabD = sb("tabD", [P, 3, NT, 4], BF16)
    hn = sb("hn", [P, NT, 16])
    anode = sb("anode", [P, 2, NT, 4])
    peak = sb("peak", [P, 8])
    peakT = sb("peakT", [8, 16])
    peakB = sb("peakB", [P, 8])
    trips = sb("trips", [P, 1], I32)
    agg = sb("agg", [P, NT, SV])
    sg = sb("sg", [P, 4, NT, 4])
    ones8 = sb("ones8", [8, P])
    g_tensor = Signal(ctx, nc, "graph_tensor_done")
    g_scalar = Signal(ctx, nc, "graph_scalar_done")
    g_vector = Signal(ctx, nc, "graph_vector_done")
    g_pool = Signal(ctx, nc, "graph_pool_done")
    edges_in = Signal(ctx, nc, "edges_in")

    def leaky(v, out, x):
        return v.scalar_tensor_tensor(out=out, in0=x, scalar=0.2, in1=x, op0=ALU.mult, op1=ALU.max)

    def vector_steps(steps, waits={}):
        with stage(dve=len(steps)) as (block, tallies):
            @block.vector
            def _(eng):
                _, _, dve, _ = tallies()
                for f in steps:
                    f(nc.vector).then_inc(dve.up(), 1)
                    eng.wait_ge(vector_done.sem, dve.at(dve.k))

    def graph_nodes():
        projected([(XT, w("g_w"))], 16, hn)
        h4 = lambda: R[:, :, 0:16].rearrange("p t (h e) -> p t h e", e=4)
        steps = []
        for k, name in ((0, "g_att_src"), (1, "g_att_dst")):
            steps.append(lambda v, name=name: v.tensor_tensor(R[:, :, 0:16], hn[:], bc(row(name), 1, NT), ALU.mult))
            steps.append(lambda v, k=k: v.reduce_sum(anode[:, k], h4(), axis=AX.X))
        for tab, src, n in ((tabS, hn[:], HV), (tabD, anode[:, 1], 4)):
            rest = R[:, :, 0:n]
            steps.append(lambda v, tab=tab, src=src: v.tensor_copy(tab[:, 0], src))
            steps.append(lambda v, tab=tab, src=src, rest=rest: v.tensor_tensor(rest, src, tab[:, 0], ALU.subtract))
            steps.append(lambda v, tab=tab, rest=rest: v.tensor_copy(tab[:, 1], rest))
            steps.append(lambda v, tab=tab, rest=rest: v.tensor_tensor(rest, rest, tab[:, 1], ALU.subtract))
            steps.append(lambda v, tab=tab, rest=rest: v.tensor_copy(tab[:, 2], rest))
        vector_steps(steps)

    def graph_edges():
        with stage() as (block, tallies):
            @block.sync
            def _(eng):
                eng.dma_start(edge_src.rearrange("p a b -> p (a b)"), T["edges"][0]).then_inc(edges_in.sem, 16)
                eng.dma_start(edge_dst.rearrange("p a b -> p (a b)"), T["edges"][1]).then_inc(edges_in.sem, 16)
                eng.wait_ge(edges_in.sem, 32)
        steps = [
            lambda v: v.tensor_scalar(outside, edge_dst, float(N), None, ALU.is_ge),
            lambda v: v.tensor_tensor_scan(distance[:, 0], outside[:, 0], outside[:, 0], 0.0, ALU.add, ALU.max),
            lambda v: v.tensor_tensor_scan(distance[:, 1], outside[:, 1], outside[:, 1], 0.0, ALU.add, ALU.max),
            lambda v: v.tensor_scalar(peak[:, 4:6], distance[:, :, HALF - 1], -1.0, float(HALF), ALU.mult, ALU.add),
            lambda v: v.scalar_tensor_tensor(out=distance, in0=outside, scalar=0.0, in1=distance, op0=ALU.is_equal, op1=ALU.mult),
            lambda v: v.tensor_copy(packed[0], distance),
            lambda v: v.tensor_scalar(packed[0], packed[0], 22, None, ALU.logical_shift_left),
            lambda v: v.tensor_scalar(edge_dst, edge_dst, N - 1, 11, ALU.bitwise_and, ALU.logical_shift_left),
            lambda v: v.tensor_scalar(edge_src, edge_src, float(N - 1), None, ALU.min),
            lambda v: v.tensor_tensor(packed[0], packed[0], edge_dst, ALU.bitwise_or),
            lambda v: v.tensor_tensor(packed[0], packed[0], edge_src, ALU.bitwise_or),
        ]
        for b in range(BITS):
            a, z, n = packed[b % 2], packed[1 - b % 2], 2 ** b
            steps += [
                lambda v, a=a, b=b: v.tensor_scalar(moves, a, 22 + b, 1, ALU.logical_shift_right, ALU.bitwise_and),
                lambda v: v.tensor_scalar(stays, moves, 1.0, None, ALU.subtract),
                lambda v, a=a, z=z: v.tensor_tensor(z, a, stays, ALU.bitwise_and),
                lambda v, a=a, z=z, n=n: v.copy_predicated(z[:, :, 0:HALF - n], moves[:, :, n:HALF], a[:, :, n:HALF]),
            ]
        last = packed[BITS % 2]
        for dst, shift, bits in ((srclo, 0, 127), (srchi, 7, 15), (dstlo, 11, 127), (dsthi, 18, 15)):
            by_half = dst[:, 0:2 * HALF].rearrange("p (c a) -> p a c", a=2)
            steps += [
                lambda v, shift=shift, bits=bits: v.tensor_scalar(field, last, shift, bits, ALU.logical_shift_right, ALU.bitwise_and),
                lambda v, by_half=by_half: v.tensor_copy(by_half, field),
                lambda v, dst=dst: v.memset(dst[:, 2 * HALF:2 * COLS], 64.0),
            ]
        by_half = dsthi[:, 0:2 * HALF].rearrange("p (c a) -> p a c", a=2)
        pad = part(2048, [2, HALF])
        cols = part(0, [HALF]) if BITS % 2 == 0 else part(4096, [HALF])
        assert BITS % 2 == 0
        vector_steps(steps)
        with stage(pool=1) as (block, tallies):
            @block.gpsimd
            def _(eng):
                pool = tallies()[3]
                eng.iota(cols.bitcast(I32), pattern=[[1, HALF]], base=0, channel_multiplier=0).then_inc(pool.up(), 1)
        vector_steps([
            lambda v: v.tensor_scalar(pad[:, 0], cols.bitcast(I32), peak[:, 4:5], 64.0, ALU.is_ge, ALU.mult),
            lambda v: v.tensor_scalar(pad[:, 1], cols.bitcast(I32), peak[:, 5:6], 64.0, ALU.is_ge, ALU.mult),
            lambda v: v.tensor_tensor(by_half, by_half, pad, ALU.add),
        ])

    def graph_peaks():
        vector_steps([lambda v: v.reduce_max(peak[:, 0:4], anode[:, 0].rearrange("p t h -> p h t"), axis=AX.X),
                      lambda v: v.memset(ones8[:], 1.0)])
        with stage(pe=2, dve=4) as (block, tallies):
            @block.tensor
            def _(eng):
                pe, _, dve, _ = tallies()
                nc.tensor.transpose(PS[0:6, 0, 0:P], peak[:, 0:6], ident).then_inc(pe.up(), 1)
                eng.wait_ge(vector_done.sem, dve.at(2))
                nc.tensor.matmul(PS[:, 1, 0:6], ones8[0:6, :], peakT[0:6, 8:14], start=True, stop=True).then_inc(pe.up(), 1)

            @block.vector
            def _(eng):
                pe, _, dve, _ = tallies()
                eng.wait_ge(tensor_done.sem, pe.at(1))
                nc.vector.reduce_max(peakT[0:6, 0:1], PS[0:6, 0, 0:P], axis=AX.X).then_inc(dve.up(), 1)
                eng.wait_ge(vector_done.sem, dve.at(1))
                nc.vector.tensor_scalar(peakT[0:6, 8:14], ident[0:6, 0:6], peakT[0:6, 0:1], None, ALU.mult).then_inc(dve.up(), 1)
                eng.wait_ge(tensor_done.sem, pe.at(2))
                nc.vector.tensor_copy(peakB[:, 0:6], PS[:, 1, 0:6]).then_inc(dve.up(), 1)
                eng.wait_ge(vector_done.sem, dve.at(3))
                nc.vector.tensor_tensor(trips[:], peakB[:, 4:5], peakB[:, 5:6], ALU.max).then_inc(dve.up(), 1)

    VS, PS_, AS, LS = 16, 3, 3, 1

    def one_hots(v, t, par2, par4):
        at = bass.ds(t * C4, C4) if not isinstance(t, int) else slice(t * C4, (t + 1) * C4)
        iota = bc(C["iota"], 1, C4)
        hi = bc(C["hi"], 1, C4)
        return [
            lambda: v.tensor_tensor(OHs[:, par2], iota, bc(srclo[:, at], 2, P), ALU.is_equal),
            lambda: v.tensor_tensor(OHd[:, par4], iota, bc(dstlo[:, at], 2, P), ALU.is_equal),
            lambda: v.tensor_tensor(maskS[:, par2], hi, bc(srchi[:, at], 2, 16), ALU.is_equal),
            lambda: v.tensor_tensor(maskD[:, par4], hi, bc(dsthi[:, at], 2, 16), ALU.is_equal),
        ]

    def graph_start():
        vector_steps([
            lambda v: v.memset(part(512, [2048]), 0.0),
            lambda v: v.memset(spread.rearrange("p a c h v -> p (a c h v)"), 0.0),
            lambda v: v.memset(maskS[:], 0.0),
            lambda v: v.memset(maskD[:], 0.0),
            lambda v: v.memset(vals[:], 0.0),
            lambda v: v.memset(PS[:, 0:4, :], 0.0),
        ] + [lambda v, f=f: f() for f in one_hots(nc.vector, 0, 0, 0)])
        with nc.Block() as block:
            @block.tensor
            def _(eng):
                eng.matmul(PS[:, 4, 0:16 * SV], OHd[:, 1, 0, :], spread[:, 0, 0].rearrange("p h v -> p (h v)"),
                           start=True, stop=True, skip_group_check=True).then_inc(g_tensor.sem, LAG * PS_)

            @block.vector
            def _(eng):
                eng.memset(sm[0], 0.0).then_inc(g_vector.sem, LAG * VS)

            @block.scalar
            def _(eng):
                eng.activation(peak[:, 7:8], peak[:, 0:1], ACT.Copy).then_inc(g_scalar.sem, LAG * AS)

            @block.gpsimd
            def _(eng):
                eng.memset(sm[1], 0.0).then_inc(g_pool.sem, LAG * LS)

    def graph_sums():
        def at(i, s, back, k, per):
            return i * (4 * per) + ((s - back + LAG) * per + k)

        last_trip = (HALF // 2 + 2) // 4 + 1

        def trip(eng, f):
            n = eng.value_load(trips[0:1, 0:1], min_val=0, max_val=HALF)
            with eng.Fori(0, last_trip) as i:
                with eng.If(i * 8 < n + 6):
                    f(i)

        with nc.Block() as block:
            @block.tensor
            def _(eng):
                def f(i):
                    for s in range(4):
                        V = lambda back, k: at(i, s, back, k, VS)
                        A = lambda back, k: at(i, s, back, k, AS)
                        eng.wait_ge(g_scalar.sem, A(1, 2))
                        eng.wait_ge(g_vector.sem, V(1, 4))
                        for c in range(C4):
                            nc.tensor.transpose(PSh[:, 5, c * P:(c + 1) * P], OHs[:, s % 2, c], identh[:])
                        for c in range(C4):
                            ins = nc.tensor.transpose(PS[:, 6, c * P:(c + 1) * P], OHd[:, s, c], ident)
                        ins.then_inc(g_tensor.sem, 1)
                        eng.wait_ge(g_pool.sem, at(i, s, 1, 1, LS))
                        for c in range(C4):
                            ins = nc.tensor.matmul(PS[:, 4, 0:16 * SV], OHd[:, (s - 3) % 4, c], spread[:, (s - 3) % 2, c].rearrange("p h v -> p (h v)"),
                                                   start=False, stop=False, skip_group_check=True)
                        ins.then_inc(g_tensor.sem, 1)
                        eng.wait_ge(g_scalar.sem, A(0, 2))
                        eng.wait_ge(g_vector.sem, V(0, 2))
                        for c in range(C4):
                            for k in range(3):
                                nc.tensor.matmul(PS[:, c, 0:16 * HV], OHsT[:, s % 2, c], tabS[:, k].rearrange("p h v -> p (h v)"), start=(k == 0), stop=(k == 2))
                            for k in range(3):
                                ins = nc.tensor.matmul(PS[:, c, 16 * HV:16 * (HV + 4)], OHdT[:, s % 2, c], tabD[:, k].rearrange("p h v -> p (h v)"), start=(k == 0), stop=(k == 2))
                        ins.then_inc(g_tensor.sem, 1)
                trip(eng, f)

            @block.scalar
            def _(eng):
                def f(i):
                    for s in range(4):
                        eng.wait_ge(g_tensor.sem, at(i, s, 0, 1, PS_))
                        nc.scalar.copy(OHsT[:, s % 2], PSh[:, 5, 0:C4 * P].rearrange("p (c n) -> p c n", n=P)).then_inc(g_scalar.sem, 1)
                        nc.scalar.copy(OHdT[:, s % 2], PS[:, 6, :].rearrange("p (c n) -> p c n", n=P)).then_inc(g_scalar.sem, 1)
                        eng.wait_ge(g_vector.sem, at(i, s, 0, 15, VS))
                        nc.scalar.activation(vals[:, (s - 1) % 2, :, HV:SV], sm[5], ACT.Exp).then_inc(g_scalar.sem, 1)
                trip(eng, f)

            @block.gpsimd
            def _(eng):
                def f(i):
                    for s in range(4):
                        eng.wait_ge(g_vector.sem, at(i, s, 0, 16, VS))
                        eng.wait_ge(g_tensor.sem, at(i, s, 1, 2, PS_))
                        m = maskD[:, (s - 2) % 4].unsqueeze(3).to_broadcast([P, C4, 16, SV])
                        x = vals[:, (s - 2) % 2].unsqueeze(2).to_broadcast([P, C4, 16, SV])
                        nc.gpsimd.tensor_tensor(spread[:, (s - 2) % 2], m, x, ALU.mult).then_inc(g_pool.sem, 1)
                trip(eng, f)

            @block.vector
            def _(eng):
                v = nc.vector

                def f(i):
                    for s in range(4):
                        k = [0]

                        def own():
                            eng.wait_ge(g_vector.sem, at(i, s, 0, k[0], VS))

                        def step(ins):
                            ins.then_inc(g_vector.sem, 1)
                            k[0] += 1

                        own()
                        eng.wait_ge(g_tensor.sem, at(i, s, 1, 3, PS_))
                        g = PS[:, 0:C4, 0:16 * HV].rearrange("p c (h v) -> p c h v", h=16)
                        step(v.tensor_tensor(pickS, g, maskS[:, (s - 1) % 2].unsqueeze(3).to_broadcast([P, C4, 16, HV]), ALU.mult))
                        g = PS[:, 0:C4, 16 * HV:16 * (HV + 4)].rearrange("p c (h v) -> p c h v", h=16)
                        step(v.tensor_tensor(pickD, g, maskD[:, (s - 1) % 4].unsqueeze(3).to_broadcast([P, C4, 16, 4]), ALU.mult))
                        own()
                        eng.wait_ge(g_tensor.sem, at(i, s, 0, 2, PS_))
                        eng.wait_ge(g_pool.sem, at(i, s, 1, 1, LS))
                        for hot in one_hots(v, i * 4 + (s + 1), (s + 1) % 2, (s + 1) % 4):
                            step(hot())
                        step(v.reduce_sum(vals[:, (s - 1) % 2, :, 0:HV], pickS.rearrange("p c h v -> p c v h"), axis=AX.X))
                        step(v.reduce_sum(sm[0], pickD.rearrange("p c h v -> p c v h"), axis=AX.X))
                        own()
                        step(v.tensor_tensor(hatt, vals[:, (s - 1) % 2, :, 0:HV], bc(row("g_att_src"), 1, C4), ALU.mult))
                        own()
                        step(v.reduce_sum(sm[1], hatt.rearrange("p c (h e) -> p c h e", e=4), axis=AX.X))
                        own()
                        step(v.tensor_tensor(sm[1], sm[1], sm[0], ALU.add))
                        step(v.tensor_tensor(sm[2], sm[0], bc(peakB[:, 0:4], 1, C4), ALU.add))
                        own()
                        step(leaky(v, sm[3], sm[1]))
                        step(leaky(v, sm[4], sm[2]))
                        own()
                        eng.wait_ge(g_scalar.sem, at(i, s, 1, 3, AS))
                        step(v.tensor_tensor(sm[5], sm[3], sm[4], ALU.subtract))
                        x = vals[:, (s - 2) % 2]
                        weight = x[:, :, HV:SV].unsqueeze(3).to_broadcast([P, C4, 4, 4])
                        feats = x[:, :, 0:HV].rearrange("p c (h e) -> p c h e", e=4)
                        step(v.tensor_tensor(feats, feats, weight, ALU.mult))
                        assert k[0] == VS
                trip(eng, f)

    def l1_ffn():
        normalised(H, X, turned=XT)
        graph_nodes()
        graph_edges()
        graph_peaks()
        graph_start()
        graph_sums()
        with stage(dve=3 + 3, act=1) as (block, tallies):
            @block.vector
            def _(eng):
                _, act, dve, _ = tallies()
                v = nc.vector

                def step(ins):
                    ins.then_inc(dve.up(), 1)
                    eng.wait_ge(vector_done.sem, dve.at(dve.k))

                step(v.tensor_tensor(sg[:, 0], anode[:, 0], anode[:, 1], ALU.add))
                step(v.tensor_tensor(sg[:, 1], anode[:, 1], bc(peakB[:, 0:4], 1, NT), ALU.add))
                step(leaky(v, sg[:, 2], sg[:, 0]))
                step(leaky(v, sg[:, 3], sg[:, 1]))
                step(v.tensor_tensor(sg[:, 0], sg[:, 2], sg[:, 3], ALU.subtract))
                step(v.tensor_copy(agg[:], PS[:, 4, 0:16 * SV].rearrange("p (t v) -> p t v", v=SV)))

            @block.scalar
            def _(eng):
                _, act, dve, _ = tallies()
                eng.wait_ge(vector_done.sem, dve.at(5))
                nc.scalar.activation(sg[:, 1], sg[:, 0], ACT.Exp).then_inc(act.up(), 1)
        own = R[:, :, 0:16]
        own4 = own.rearrange("p t (h e) -> p t h e", e=4)
        feats = agg[:, :, 0:HV]
        feats4 = feats.rearrange("p t (h e) -> p t h e", e=4)
        up4 = lambda x: x.unsqueeze(3).to_broadcast([P, NT, 4, 4])
        s0, s1 = st[:, 0, :], st[:, 1, :]
        vector_steps([
            lambda v: v.tensor_tensor(own4, hn[:].rearrange("p t (h e) -> p t h e", e=4), up4(sg[:, 1]), ALU.mult),
            lambda v: v.tensor_tensor(feats, feats, own, ALU.add),
            lambda v: v.tensor_tensor(sg[:, 2], agg[:, :, HV:SV], sg[:, 1], ALU.add),
            lambda v: v.scalar_tensor_tensor(out=sg[:, 2], in0=sg[:, 1], scalar=1e-16, in1=sg[:, 2], op0=ALU.mult, op1=ALU.add),
            lambda v: v.reciprocal(sg[:, 3], sg[:, 2]),
            lambda v: v.tensor_tensor(feats4, feats4, up4(sg[:, 3]), ALU.mult),
            lambda v: v.tensor_tensor(feats, feats, bc(row("g_b_gat"), 1, NT), ALU.add),
            lambda v: v.reduce_sum(s0, feats, axis=AX.X),
            lambda v: v.tensor_scalar(s0, s0, 1.0 / 16, None, ALU.mult),
            lambda v: v.tensor_tensor(feats, feats, bc(s0, 2, 16), ALU.subtract),
            lambda v: v.tensor_tensor(own, feats, feats, ALU.mult),
            lambda v: v.reduce_sum(s1, own, axis=AX.X),
            lambda v: v.tensor_scalar(s1, s1, 1.0 / 16, LN_EPS, ALU.mult, ALU.add),
        ])
        with stage(act=1) as (block, tallies):
            @block.scalar
            def _(eng):
                _, act, _, _ = tallies()
                nc.scalar.activation(st[:, 2, :], s1, ACT.Sqrt).then_inc(act.up(), 1)
        vector_steps([
            lambda v: v.reciprocal(st[:, 3, :], st[:, 2, :]),
            lambda v: v.tensor_tensor(feats, feats, bc(st[:, 3, :], 2, 16), ALU.mult),
            lambda v: v.tensor_tensor(feats, feats, bc(row("g_ln_gamma"), 1, NT), ALU.mult),
            lambda v: v.tensor_tensor(feats, feats, bc(row("g_ln_beta"), 1, NT), ALU.add),
            lambda v: v.reduce_sum(sg[:, 0], feats.rearrange("p t (h e) -> p t e h", e=4), axis=AX.X),
            lambda v: v.tensor_scalar(L16[:, :, 0:4], sg[:, 0], 0.25, None, ALU.mult),
        ])
        top2_gates(4)
        transposed(G16[:, :, 0:4], GT[0:4], 4)
        projected([(GT[0:4], w("f1_b2"))], D, H, add=H)
        experts(4, [P], lambda e, f: w("f1_w1")[:, e * P:(e + 1) * P], lambda e, j, f: w("f1_w2")[:, e * D:(e + 1) * D],
                ACT.Gelu, H, b1=lambda e, f: w("f1_b1")[:, e:e + 1])

    def channel_norm(Z, gamma, beta, eps=1e-5):
        z = Z[:].rearrange("p t (h d) -> p (t h) d", d=4)
        a4 = tA[:].rearrange("p t (h d) -> p (t h) d", d=4)
        b4 = tB[:].rearrange("p t (h d) -> p (t h) d", d=4)
        with stage(act=1, dve=11) as (block, tallies):
            @block.vector
            def _(eng):
                _, act, dve, _ = tallies()
                v = nc.vector

                def step(ins):
                    ins.then_inc(dve.up(), 1)
                    eng.wait_ge(vector_done.sem, dve.at(dve.k))

                step(v.reduce_sum(chan[:, 0, :], z, axis=AX.X))
                step(v.tensor_scalar(chan[:, 0, :], chan[:, 0, :], 0.25, None, ALU.mult))
                step(v.tensor_tensor(a4, z, bc(chan[:, 0, :], 2, 4), ALU.subtract))
                step(v.tensor_tensor(b4, a4, a4, ALU.mult))
                step(v.reduce_sum(chan[:, 1, :], b4, axis=AX.X))
                step(v.tensor_scalar(chan[:, 1, :], chan[:, 1, :], 1.0 / 3.0, None, ALU.mult))
                eng.wait_ge(scalar_done.sem, act.at(1))
                step(v.tensor_scalar(chan[:, 2, :], chan[:, 2, :], eps, None, ALU.add))
                step(v.reciprocal(chan[:, 2, :], chan[:, 2, :]))
                step(v.tensor_tensor(a4, a4, bc(chan[:, 2, :], 2, 4), ALU.mult))
                step(v.tensor_tensor(tA[:], tA[:], bc(gamma, 1, NT), ALU.mult))
                step(v.tensor_tensor(Z[:], tA[:], bc(beta, 1, NT), ALU.add))

            @block.scalar
            def _(eng):
                _, act, dve, _ = tallies()
                eng.wait_ge(vector_done.sem, dve.at(6))
                nc.scalar.activation(chan[:, 2, :], chan[:, 1, :], ACT.Sqrt).then_inc(act.up(), 1)

    chan = sb("chan", [P, 3, NT * 16])

    def l2_attn():
        normalised(H, X, turned=XT)
        projected([(XT, w("a2_wk"))], D, Y, bias=row("a2_bk"))
        projected([(XT, w("a2_wv"))], D, R, bias=row("a2_bv"))
        channel_norm(Y, row("a2_kln_w"), row("a2_kln_b"))
        channel_norm(R, row("a2_vln_w"), row("a2_vln_b"))
        with stage(pe=1, dve=1) as (block, tallies):
            @block.tensor
            def _(eng):
                pe, _, _, _ = tallies()
                for b in range(B):
                    for t in range(TB):
                        ins = nc.tensor.matmul(PS[0:D, 0, b * D:(b + 1) * D], Y[:, b * TB + t, :], R[:, b * TB + t, :], start=(t == 0), stop=(t == TB - 1))
                ins.then_inc(pe.up(), 1)

            @block.vector
            def _(eng):
                pe, _, dve, _ = tallies()
                eng.wait_ge(tensor_done.sem, pe.at(1))
                nc.vector.tensor_tensor(KVm[:], PS[0:D, 0, 0:B * D].rearrange("p (b n) -> p b n", n=D), bc(C["heads"][0:D], 1, B), ALU.mult).then_inc(dve.up(), 1)
        features(w("a2_wq"), XT, ET[:], bias=w("a2_bq"))
        projected([(ET, lambda t: KVm[:, t // TB, :])], D, Y, add=X)
        transposed(Y, ET)
        projected([(ET, w("a2_wp"))], D, Y, bias=row("a2_bp"))
        with stage(act=1, dve=2) as (block, tallies):
            @block.scalar
            def _(eng):
                _, act, _, _ = tallies()
                nc.scalar.activation(Y[:], Y[:], ACT.Gelu).then_inc(act.up(), 1)

            @block.vector
            def _(eng):
                _, act, dve, _ = tallies()
                nc.vector.tensor_tensor(H[:], H[:], X[:], ALU.add).then_inc(dve.up(), 1)
                eng.wait_ge(scalar_done.sem, act.at(1))
                eng.wait_ge(vector_done.sem, dve.at(1))
                nc.vector.tensor_tensor(H[:], H[:], Y[:], ALU.add).then_inc(dve.up(), 1)

    def l2_ffn():
        normalised(H, X, turned=XT)
        projected([(XT, w("f2_router"))], 8, L16[:, :, 0:8])
        top2_gates(8)
        transposed(G16[:, :, 0:8], GT[0:8], 8)
        summed(H, H, X)
        projected([(GT[0:8], w("f2_b2"))], D, H, add=H)
        experts(8, [P], lambda g, f: w("f2_w1")[:, g * P:(g + 1) * P], lambda g, j, f: w("f2_w2")[j * D:(j + 1) * D, g * D:(g + 1) * D],
                ACT.Gelu, H, b1=lambda g, f: w("f2_b1")[:, g:g + 1], share=2)

    def l3_attn():
        normalised(H, X, turned=XT)
        q, k = w("a3_wq"), w("a3_wk")
        softmax_attention(8, KD, [q[:, 0:P], q[:, P:2 * P]], [k[:, 0:P], k[:, P:2 * P]], w("a3_vo"), H, 1.0 / 8.0)

    def l3_ffn():
        normalised(H, X)
        normalised(X, R, eps=1e-6, center=False, gamma=row("f3_ln1"), turned=XT)
        weight_products([(w("f3_wv")[:, (h // 2) * D:(h // 2 + 1) * D], w("f3_wo")[:, h * D:(h + 1) * D]) for h in range(4)], MV, D)
        softmax_attention(4, KD, [(w("f3_wq")[:, 0:P], w("f3_wq")[:, P:2 * P])], [(w("f3_wk")[:, 0:P], w("f3_wk")[:, P:2 * P])],
                          MV[:, 0:4 * D], X, 0.25, causal=True, rope=(C["cos"], C["sin"]))
        normalised(X, R, eps=1e-6, center=False, gamma=row("f3_ln2"), turned=XT)
        projected([(XT, w("f3_router"))], 8, L16[:, :, 0:8])
        top2_gates(8, eps=1e-9)
        F = 85
        experts(8, [F, F], lambda e, f: w("f3_w1")[:, (2 * e + f) * F:(2 * e + f + 1) * F],
                lambda e, j, f: w("f3_w2")[:, (2 * e + f) * D:(2 * e + f + 1) * D], ACT.Silu, X,
                w3=lambda e, f: w("f3_w3")[:, (2 * e + f) * F:(2 * e + f + 1) * F])
        summed(H, H, X)

    l0_attn()
    l0_ffn()
    l1_attn()
    l1_ffn()
    l2_attn()
    l2_ffn()
    l3_attn()
    l3_ffn()

    with stage() as (block, tallies):
        @block.sync
        def _(eng):
            eng.dma_start(out.rearrange("b (t p) d -> p (b t) d", p=P), H[:]).then_inc(written.sem, 16)
            eng.wait_ge(written.sem, 16)


def laid_out(i):
    g = lambda n: np.asarray(i[n])
    o = {}
    f = {}
    o["consts"] = constants()
    o["ids"] = g("x").astype(np.int32).reshape(N)
    pairs = lambda a: np.ascontiguousarray(a.reshape(B, S, TB, P).transpose(3, 0, 2, 1).reshape(P, NT, S))
    o["rel"] = pairs(g("fside_BSS_rel_dist"))
    o["adj"] = pairs(g("mask_BSS_b0_1").view(np.uint8)).view(np.int32)
    ex = lambda a: a.transpose(1, 0, 2).reshape(a.shape[1], -1)
    W = {}
    R = {}
    W["atom_embed"], W["neighbor_embed"] = g("L0_tok_atom_embed"), g("L0_tok_neighbor_embed")
    W["w_rd"] = g("L0_tok_w_rd")[:, None]
    W["tok_w1a"], W["tok_w1b"], W["tok_w2"] = g("L0_tok_w1")[:D], g("L0_tok_w1")[D:], g("L0_tok_w2")
    R["tok_b1"], R["tok_gamma"], R["tok_beta"], R["tok_b2"] = g("L0_tok_b1"), g("L0_tok_gamma"), g("L0_tok_beta"), g("L0_tok_b2")
    W["a0_wq"], W["a0_wk"], W["a0_wo"] = ex(g("L0_attn_Wqs")), ex(g("L0_attn_Wks")), ex(g("L0_attn_Wo"))
    W["a0_wvT"] = ex(g("L0_attn_Wvs").transpose(0, 2, 1))
    W["f0_gate"], R["f0_gate_b"] = g("L0_ffn_gate_w"), g("L0_ffn_gate_b")
    W["f0_w1"], W["f0_w2"], W["f0_b1"], W["f0_b2"] = ex(g("L0_ffn_w1")), ex(g("L0_ffn_w2")), g("L0_ffn_b1").T, g("L0_ffn_b2")
    R["f0_gamma"], R["f0_beta"] = g("L0_ffn_gamma"), g("L0_ffn_beta")
    twice = lambda a: np.concatenate([a, a], axis=1)
    W["a1_wq"], W["a1_wk"], W["a1_wv"] = twice(g("L1_attn_Wq").T), twice(g("L1_attn_Wk").T), g("L1_attn_Wv").T
    qkv = g("L2_attn_W_qkv").reshape(16, 3, 4, D)
    bq = g("L2_attn_b_qkv").reshape(16, 3, 4)
    for n, k in (("q", 0), ("k", 1), ("v", 2)):
        W["a2_w" + n] = qkv[:, k].reshape(D, D).T
    W["a2_bq"] = bq[:, 0].reshape(D, 1)
    R["a2_bk"], R["a2_bv"] = bq[:, 1].reshape(D), bq[:, 2].reshape(D)
    for n in ("kln_w", "kln_b", "vln_w", "vln_b"):
        R["a2_" + n] = g("L2_attn_" + n).reshape(D)
    W["a2_wp"], R["a2_bp"] = g("L2_attn_W_proj").T, g("L2_attn_b_proj")
    W["f2_router"] = g("L2_ffn_router_w").T
    W["f2_w1"], W["f2_b2"] = ex(g("L2_ffn_w1")), g("L2_ffn_b2")
    W["f2_w2"] = g("L2_ffn_w2").reshape(4, P, D).transpose(1, 0, 2).reshape(P, 4 * D)
    W["f2_b1"] = g("L2_ffn_b1").reshape(4, P).T
    W["a3_wq"], W["a3_wk"] = (g("L3_attn_" + n).transpose(2, 0, 1).reshape(D, -1) for n in "QK")
    W["a3_vo"] = ex(g("L3_attn_VO"))
    HD = 16
    swap = np.r_[HD // 2:HD, 0:HD // 2]

    def rope_rows(w, heads, each):
        w = np.repeat(w.reshape(heads, HD, D), each, axis=0)
        z = np.zeros((2, 4, KD, D), np.float32)
        z[0, :, :HD], z[1, :, :HD] = w, w[:, swap]
        return z.reshape(2 * P, D).T

    W["f3_wq"], W["f3_wk"] = rope_rows(g("L3_ffn_wq"), 4, 1), rope_rows(g("L3_ffn_wk"), 2, 2)
    W["f3_wv"] = g("L3_ffn_wv").reshape(2, HD, D).transpose(1, 0, 2).reshape(HD, 2 * D)
    W["f3_wo"] = g("L3_ffn_wo").reshape(D, 4, HD).transpose(2, 1, 0).reshape(HD, 4 * D)
    R["f3_ln1"], R["f3_ln2"] = g("L3_ffn_ln1_w"), g("L3_ffn_ln2_w")
    W["f3_router"] = g("L3_ffn_router_w").T
    W["f3_w1"], W["f3_w3"] = (g("L3_ffn_" + n).transpose(2, 0, 1).reshape(D, -1) for n in ("w1", "w3"))
    F = 85
    W["f3_w2"] = g("L3_ffn_w2").reshape(8, D, 2, F).transpose(3, 0, 2, 1).reshape(F, -1)
    W["g_w"] = g("L1_ffn_W_gat")
    R["g_att_src"], R["g_att_dst"] = g("L1_ffn_att_src").reshape(16), g("L1_ffn_att_dst").reshape(16)
    for n in ("b_gat", "ln_gamma", "ln_beta"):
        R["g_" + n] = g("L1_ffn_" + n)
    W["f1_w1"], W["f1_w2"], W["f1_b1"], W["f1_b2"] = ex(g("L1_ffn_W1")), ex(g("L1_ffn_W2")), g("L1_ffn_b1").T, g("L1_ffn_b2")
    o["edges"] = g("L1_ffn_edge_index").astype(np.int32).reshape(2, P, EDGES // P)
    o |= {"w_" + n: a for n, a in W.items()}
    o |= {"r_" + n: a for n, a in R.items()}
    return {n: np.ascontiguousarray(a) for n, a in o.items()}


def kernel(**inputs):
    import concourse.bacc as bacc
    from concourse.bass_utils import run_bass_kernel_spmd

    nc = bacc.Bacc("TRN2", target_bir_lowering=False, num_devices=1)
    arrays = laid_out(inputs)
    T = {n: nc.dram_tensor("in_" + n, list(a.shape), mybir.dt.from_np(a.dtype), kind="ExternalInput").ap() for n, a in arrays.items()}
    out = nc.dram_tensor("out", [B, S, D], F32, kind="ExternalOutput").ap()
    program(nc, T, out)
    r = run_bass_kernel_spmd(nc, [{"in_" + n: a for n, a in arrays.items()}], core_ids=[0])
    return r.results[0]["out"]
```
